# Optimizing a Trainium2 kernel written in Bass

```python
import numpy as np
import jax
import jax.numpy as jnp

def _softmax(x, axis=-1):
    return jax.nn.softmax(x, axis=axis)

def _gelu(x):
    return jax.nn.gelu(x, approximate=True)

def _silu(x):
    return jax.nn.silu(x)

def _sigmoid(x):
    return jax.nn.sigmoid(x)

def _layernorm(x, axis=-1, eps=1e-05):
    m = jnp.mean(x, axis=axis, keepdims=True)
    v = jnp.var(x, axis=axis, keepdims=True)
    return (x - m) / jnp.sqrt(v + eps)

def _scatter_add(tgt, idx, src, axis=0):
    return tgt.at[idx].add(src)

def _segment_sum(src, seg, n):
    return jax.ops.segment_sum(src, seg, n)
kernel_name = 'mk_dlrm_tower_d1_rec_r8_4a34a4'

def setup_inputs(seed: int=0):
    np.random.seed(seed)
    _w = jnp.asarray

    def _rec_inputs():
        import jax
        import jax.numpy as jnp
        _tk = jax.random.key(seed)
        dense_ctx = jax.random.normal(jax.random.fold_in(_tk, 190), (512, 16), jnp.float32)
        ids = jnp.stack([jax.random.randint(jax.random.fold_in(_tk, 200 + f), (512,), 0, v, jnp.int32) for f, v in enumerate([1250, 1250, 125000, 1250, 125000, 12500, 125000, 125000, 12500, 1250, 1000, 1250, 12500, 1250, 1000, 1250, 1000, 1250, 1000, 12500, 1000, 1000, 1000, 1250, 1000, 12500])], axis=1)
        tbl_0 = 0.05 * jax.random.normal(jax.random.fold_in(_tk, 500 + 0), (1250, 32), jnp.float32)
        tbl_1 = 0.05 * jax.random.normal(jax.random.fold_in(_tk, 500 + 1), (1250, 32), jnp.float32)
        tbl_2 = 0.05 * jax.random.normal(jax.random.fold_in(_tk, 500 + 2), (125000, 32), jnp.float32)
        tbl_3 = 0.05 * jax.random.normal(jax.random.fold_in(_tk, 500 + 3), (1250, 32), jnp.float32)
        tbl_4 = 0.05 * jax.random.normal(jax.random.fold_in(_tk, 500 + 4), (125000, 32), jnp.float32)
        tbl_5 = 0.05 * jax.random.normal(jax.random.fold_in(_tk, 500 + 5), (12500, 32), jnp.float32)
        tbl_6 = 0.05 * jax.random.normal(jax.random.fold_in(_tk, 500 + 6), (125000, 32), jnp.float32)
        tbl_7 = 0.05 * jax.random.normal(jax.random.fold_in(_tk, 500 + 7), (125000, 32), jnp.float32)
        tbl_8 = 0.05 * jax.random.normal(jax.random.fold_in(_tk, 500 + 8), (12500, 32), jnp.float32)
        tbl_9 = 0.05 * jax.random.normal(jax.random.fold_in(_tk, 500 + 9), (1250, 32), jnp.float32)
        tbl_10 = 0.05 * jax.random.normal(jax.random.fold_in(_tk, 500 + 10), (1000, 32), jnp.float32)
        tbl_11 = 0.05 * jax.random.normal(jax.random.fold_in(_tk, 500 + 11), (1250, 32), jnp.float32)
        tbl_12 = 0.05 * jax.random.normal(jax.random.fold_in(_tk, 500 + 12), (12500, 32), jnp.float32)
        tbl_13 = 0.05 * jax.random.normal(jax.random.fold_in(_tk, 500 + 13), (1250, 32), jnp.float32)
        tbl_14 = 0.05 * jax.random.normal(jax.random.fold_in(_tk, 500 + 14), (1000, 32), jnp.float32)
        tbl_15 = 0.05 * jax.random.normal(jax.random.fold_in(_tk, 500 + 15), (1250, 32), jnp.float32)
        tbl_16 = 0.05 * jax.random.normal(jax.random.fold_in(_tk, 500 + 16), (1000, 32), jnp.float32)
        tbl_17 = 0.05 * jax.random.normal(jax.random.fold_in(_tk, 500 + 17), (1250, 32), jnp.float32)
        tbl_18 = 0.05 * jax.random.normal(jax.random.fold_in(_tk, 500 + 18), (1000, 32), jnp.float32)
        tbl_19 = 0.05 * jax.random.normal(jax.random.fold_in(_tk, 500 + 19), (12500, 32), jnp.float32)
        tbl_20 = 0.05 * jax.random.normal(jax.random.fold_in(_tk, 500 + 20), (1000, 32), jnp.float32)
        tbl_21 = 0.05 * jax.random.normal(jax.random.fold_in(_tk, 500 + 21), (1000, 32), jnp.float32)
        tbl_22 = 0.05 * jax.random.normal(jax.random.fold_in(_tk, 500 + 22), (1000, 32), jnp.float32)
        tbl_23 = 0.05 * jax.random.normal(jax.random.fold_in(_tk, 500 + 23), (1250, 32), jnp.float32)
        tbl_24 = 0.05 * jax.random.normal(jax.random.fold_in(_tk, 500 + 24), (1000, 32), jnp.float32)
        tbl_25 = 0.05 * jax.random.normal(jax.random.fold_in(_tk, 500 + 25), (12500, 32), jnp.float32)
        _rk = jax.random.fold_in(_tk, 7)
        W_top1 = 0.0606339 * jax.random.normal(jax.random.fold_in(_tk, 801), (272, 512), jnp.float32)
        W_top2 = 0.0441942 * jax.random.normal(jax.random.fold_in(_tk, 802), (512, 256), jnp.float32)
        W_top3 = 0.0625 * jax.random.normal(jax.random.fold_in(_tk, 803), (256, 1), jnp.float32)
        b_top1 = jnp.zeros((512,), jnp.float32)
        b_top2 = jnp.zeros((256,), jnp.float32)
        return (dense_ctx, ids, tbl_0, tbl_1, tbl_2, tbl_3, tbl_4, tbl_5, tbl_6, tbl_7, tbl_8, tbl_9, tbl_10, tbl_11, tbl_12, tbl_13, tbl_14, tbl_15, tbl_16, tbl_17, tbl_18, tbl_19, tbl_20, tbl_21, tbl_22, tbl_23, tbl_24, tbl_25, W_top1, b_top1, W_top2, b_top2, W_top3)
    dense_ctx, ids, tbl_0, tbl_1, tbl_2, tbl_3, tbl_4, tbl_5, tbl_6, tbl_7, tbl_8, tbl_9, tbl_10, tbl_11, tbl_12, tbl_13, tbl_14, tbl_15, tbl_16, tbl_17, tbl_18, tbl_19, tbl_20, tbl_21, tbl_22, tbl_23, tbl_24, tbl_25, W_top1, b_top1, W_top2, b_top2, W_top3 = _rec_inputs()

    def _L0_rec_setup():
        import jax, jax.numpy as jnp
        import numpy as np
        M_FIELDS = 26
        H1 = 128
        H2 = 128
        BATCH = 256
        EMB_K = 32

        def _cin_layer(x_prev, x0, W, b):
            return jnp.einsum('bik,bjk,hij->bhk', x_prev, x0, W) + b[None, :, None]
        key = jax.random.key(seed)
        k0, k1, k2, k3, k4 = jax.random.split(key, 5)
        inputs = jax.random.normal(k0, (BATCH, M_FIELDS, EMB_K), dtype=jnp.float32)
        W1 = jax.random.normal(k1, (H1, M_FIELDS, M_FIELDS), dtype=jnp.float32) * 0.05
        b1 = jax.random.normal(k2, (H1,), dtype=jnp.float32) * 0.05
        W2 = jax.random.normal(k3, (H2, H1, M_FIELDS), dtype=jnp.float32) * 0.05
        b2 = jax.random.normal(k4, (H2,), dtype=jnp.float32) * 0.05
        return {'inputs': inputs, 'W1': W1, 'b1': b1, 'W2': W2, 'b2': b2}
    _L0_rec_all = _L0_rec_setup()
    _L0_rec_in = {k: v for k, v in _L0_rec_all.items() if k in ('W1', 'b1', 'W2', 'b2')}
    del _L0_rec_all
    return {'dense_ctx': dense_ctx, 'ids': ids, 'tbl_0': tbl_0, 'tbl_1': tbl_1, 'tbl_2': tbl_2, 'tbl_3': tbl_3, 'tbl_4': tbl_4, 'tbl_5': tbl_5, 'tbl_6': tbl_6, 'tbl_7': tbl_7, 'tbl_8': tbl_8, 'tbl_9': tbl_9, 'tbl_10': tbl_10, 'tbl_11': tbl_11, 'tbl_12': tbl_12, 'tbl_13': tbl_13, 'tbl_14': tbl_14, 'tbl_15': tbl_15, 'tbl_16': tbl_16, 'tbl_17': tbl_17, 'tbl_18': tbl_18, 'tbl_19': tbl_19, 'tbl_20': tbl_20, 'tbl_21': tbl_21, 'tbl_22': tbl_22, 'tbl_23': tbl_23, 'tbl_24': tbl_24, 'tbl_25': tbl_25, 'W_top1': W_top1, 'b_top1': b_top1, 'W_top2': W_top2, 'b_top2': b_top2, 'W_top3': W_top3, 'L0_rec_W1': _L0_rec_in['W1'], 'L0_rec_b1': _L0_rec_in['b1'], 'L0_rec_W2': _L0_rec_in['W2'], 'L0_rec_b2': _L0_rec_in['b2']}

def reference(dense_ctx, ids, tbl_0, tbl_1, tbl_2, tbl_3, tbl_4, tbl_5, tbl_6, tbl_7, tbl_8, tbl_9, tbl_10, tbl_11, tbl_12, tbl_13, tbl_14, tbl_15, tbl_16, tbl_17, tbl_18, tbl_19, tbl_20, tbl_21, tbl_22, tbl_23, tbl_24, tbl_25, W_top1, b_top1, W_top2, b_top2, W_top3, L0_rec_W1, L0_rec_b1, L0_rec_W2, L0_rec_b2):
    import jax
    import jax.numpy as jnp

    def _L0_rec_ref(inputs, W1, b1, W2, b2):
        import jax, jax.numpy as jnp
        import numpy as np
        M_FIELDS = 26
        H1 = 128
        H2 = 128
        BATCH = 256
        EMB_K = 32

        def _cin_layer(x_prev, x0, W, b):
            return jnp.einsum('bik,bjk,hij->bhk', x_prev, x0, W) + b[None, :, None]
        x1 = _cin_layer(inputs, inputs, W1, b1)
        x2 = _cin_layer(x1, inputs, W2, b2)
        res = jnp.concatenate([x1, x2], axis=1)
        return jnp.sum(res, axis=-1)
    e = jnp.stack([tbl_0[ids[:, 0]], tbl_1[ids[:, 1]], tbl_2[ids[:, 2]], tbl_3[ids[:, 3]], tbl_4[ids[:, 4]], tbl_5[ids[:, 5]], tbl_6[ids[:, 6]], tbl_7[ids[:, 7]], tbl_8[ids[:, 8]], tbl_9[ids[:, 9]], tbl_10[ids[:, 10]], tbl_11[ids[:, 11]], tbl_12[ids[:, 12]], tbl_13[ids[:, 13]], tbl_14[ids[:, 14]], tbl_15[ids[:, 15]], tbl_16[ids[:, 16]], tbl_17[ids[:, 17]], tbl_18[ids[:, 18]], tbl_19[ids[:, 19]], tbl_20[ids[:, 20]], tbl_21[ids[:, 21]], tbl_22[ids[:, 22]], tbl_23[ids[:, 23]], tbl_24[ids[:, 24]], tbl_25[ids[:, 25]]], axis=1)
    z = _L0_rec_ref(e, L0_rec_W1, L0_rec_b1, L0_rec_W2, L0_rec_b2)
    z = z.reshape(z.shape[0], -1)
    h = jnp.concatenate([z, dense_ctx], axis=1)
    h = jnp.maximum(h @ W_top1 + b_top1, 0.0)
    h = jnp.maximum(h @ W_top2 + b_top2, 0.0)
    y = h @ W_top3
    return y

_drawn_inputs = setup_inputs


def setup_inputs(seed=0):
    import zlib

    import numpy as np

    out = dict(_drawn_inputs(seed))
    spreads = {'b_top1': (0.0, 2.0), 'b_top2': (0.0, 0.8)}
    factors = {'tbl_0': 8.0,
     'tbl_1': 8.0,
     'tbl_2': 8.0,
     'tbl_3': 8.0,
     'tbl_4': 8.0,
     'tbl_5': 8.0,
     'tbl_6': 8.0,
     'tbl_7': 8.0,
     'tbl_8': 8.0,
     'tbl_9': 8.0,
     'tbl_10': 8.0,
     'tbl_11': 8.0,
     'tbl_12': 8.0,
     'tbl_13': 8.0,
     'tbl_14': 8.0,
     'tbl_15': 8.0,
     'tbl_16': 8.0,
     'tbl_17': 8.0,
     'tbl_18': 8.0,
     'tbl_19': 8.0,
     'tbl_20': 8.0,
     'tbl_21': 7.76,
     'tbl_22': 8.0,
     'tbl_23': 8.0,
     'tbl_24': 8.0,
     'tbl_25': 8.0,
     'L0_rec_W1': 8.0,
     'L0_rec_W2': 4.232,
     'dense_ctx': 6.13}
    for name, (base, spread) in spreads.items():
        noise = np.random.default_rng([zlib.crc32(name.encode()), seed]).standard_normal(out[name].shape)
        drawn = base * np.exp(spread * noise) if base else spread * noise
        out[name] = jnp.asarray(drawn.astype(out[name].dtype))
    for name, factor in factors.items():
        out[name] = (out[name] * factor).astype(out[name].dtype)
    return out
```

```python
from contextlib import ExitStack

import concourse.bass as bass
from concourse import mybir

ACT = mybir.ActivationFunctionType
ALU = mybir.AluOpType
F32 = mybir.dt.float32
I32 = mybir.dt.int32

P = 128
Q = 32
G = P // Q


def build(nc, dense, ids, tables, W_top1, b_top1, W_top2, b_top2, W_top3, W1, b1, W2, b2, out):
    BATCH, F = ids.shape
    E = tables[0].shape[1]
    H = W1.shape[0]
    ND = dense.shape[1]
    N1, N2 = W_top1.shape[1], W_top2.shape[1]
    M1, M2 = N1 // P, N2 // P
    TILES = BATCH // P
    assert E == Q and H == P and F == 26 and W_top1.shape[0] == 2 * H + ND

    NA, NC = 9, 8
    NAB = 2 * NA
    assert NAB + NC == F

    def tri(n):
        return n * (n + 1) // 2

    TA = tri(NA)
    XR = 2 * TA + tri(NC) + 1
    ONE = XR - 1
    AB = NA * NA
    YR = AB + NAB
    CAB = XR
    CPC = CAB + AB
    PAIRS = CPC + NAB * NC
    J = F + 1
    JY = NC + 1
    NX, NY = G * J, G * JY
    XG = 4
    YG = 8
    XU, YU = Q // XG, Q // YG
    WT, AC = 4, F
    UW = (F + WT - 1) // WT
    U1 = UW + 1 + AC

    with ExitStack() as ctx:
        def sb(name, shape, dt=F32):
            return ctx.enter_context(nc.sbuf_tensor(name, shape, dt))

        def sem(name):
            return ctx.enter_context(nc.semaphore(name))

        bank = [ctx.enter_context(nc.psum_tensor(f"bank{i}", [P, 512], F32)) for i in range(8)]
        ZB, H1A, H1B = 5, 6, 7

        ident = sb("ident", [P, P])
        ids_sb = sb("ids_sb", [P, TILES, F], I32)
        gathered = sb("gathered", [P, 2, F, E])
        xk = sb("xk", [P, 2, F, Q])
        xdiag = [sb(f"xdiag{i}", [P, G, J, Q]) for i in range(2)]
        prodx = [sb(f"prodx{i}", [P, XR, Q]) for i in range(2)]
        prody = [sb(f"prody{i}", [P, YR, Q]) for i in range(2)]
        tx = sb("tx", [P, J, P])
        ty = sb("ty", [P, JY, P])
        w1raw = sb("w1raw", [P, F, F])
        w1both = sb("w1both", [P, F, F])
        w1s = sb("w1s", [P, PAIRS])
        cw = sb("cw", [P, F, PAIRS])
        w1p = sb("w1p", [P, NC, YR])
        cx = sb("cx", [P, F, P])
        cy = sb("cy", [P, NC, P])
        zwx = sb("zwx", [P, P])
        zwab = sb("zwab", [P, P])
        zwp = sb("zwp", [P, NC, P])
        wt1 = sb("wt1", [P, 2, N1])
        wt1d = sb("wt1d", [ND, N1])
        wt2 = sb("wt2", [P, M1, N2])
        wt3 = sb("wt3", [P, M2])
        bt1 = sb("bt1", [P, M1])
        bt2 = sb("bt2", [P, M2])
        b2s = sb("b2s", [P, 2])
        dense_sb = sb("dense_sb", [P, TILES, ND])
        dense_t = sb("dense_t", [ND, TILES, Q, G])
        zs = sb("zs", [P, 2, P])
        h1s = sb("h1s", [P, M1, P])
        h2s = sb("h2s", [P, M2, P])
        ys = sb("ys", [1, TILES, G, Q])
        w2raw = tx
        w2t = xdiag[1]

        def at(t, off, *dims, rows=P, row0=0):
            width = 1
            for n in t.shape[1:]:
                width *= n
            return bass.AP(t, row0 * width + off, [[width, rows]] + [list(d) for d in dims])

        ids_loaded = sem("ids_loaded")
        w1_loaded = sem("w1_loaded")
        w2_loaded = sem("w2_loaded")
        dense_loaded = sem("dense_loaded")
        tower_loaded = sem("tower_loaded")
        ident_zero = sem("ident_zero")
        ident_ready = sem("ident_ready")
        ab_gathered = [sem(f"ab_gathered{i}") for i in range(2)]
        c_gathered = [sem(f"c_gathered{i}") for i in range(2)]
        x_transposed = sem("x_transposed")
        w1_step = sem("w1_step")
        w1_ready = sem("w1_ready")
        w1p_ready = sem("w1p_ready")
        b2_scaled = sem("b2_scaled")
        consts_ready = sem("consts_ready")
        diag1_ready = sem("diag1_ready")
        prep_filled = sem("prep_filled")
        prep_out = [sem("prep_out_act"), sem("prep_out_dve")]
        orders_added = sem("orders_added")
        diag_ready = sem("diag_ready")
        prod_ready = sem("prod_ready")
        x_filled = sem("x_filled")
        y_filled = sem("y_filled")
        x_out = sem("x_out")
        y_out = sem("y_out")
        z_done = sem("z_done")
        z_out = sem("z_out")
        h1_done = sem("h1_done")
        h1_act = sem("h1_act")
        h1_dve = sem("h1_dve")
        h2_done = sem("h2_done")
        h2_act = sem("h2_act")
        h2_dve = sem("h2_dve")
        y_done = sem("y_done")
        tile_out = sem("tile_out")
        stored = sem("stored")

        late = []
        for j0 in range(0, F, 4):
            n = min(4, F - j0)
            late.append(([at(cw, (j0 + i) * PAIRS, (1, XR)) for i in range(n)], cx[0:XR, j0:j0 + n, :], XR))
        for j0 in range(0, NC, 4):
            late.append(([at(cw, (NAB + j0 + i) * PAIRS + CAB, (1, AB)) for i in range(4)],
                         cy[0:AB, j0:j0 + 4, :], AB))
        for j0 in range(0, NC, 4):
            late.append(([w1p[:, j0 + i, :] for i in range(4)], zwp[0:YR, j0:j0 + 4, :], YR))
        late.append(([w1s[:, 0:XR]], zwx[0:XR, :], XR))
        late.append(([w1s[:, CAB:CAB + AB]], zwab[0:AB, :], AB))
        U = U1 + len(late)

        def prep_bank(u):
            return bank[u % 8] if u < U1 else bank[5 + (u - U1) % 3]

        def emptied(eng, u):
            eng.wait_ge(prep_out[u % 2], u // 2 + 1)

        def empty_prep(eng, copy, parity, lo, hi):
            for u in range(lo, hi):
                if u % 2 != parity:
                    continue
                b = prep_bank(u)
                eng.wait_ge(prep_filled, u + 1)
                if u < UW:
                    c0 = WT * u
                    n = min(WT, F - c0)
                    c = copy(at(w2t, c0 * P, (1, n * P)), b[:, 0:n * P])
                elif u == UW:
                    c = copy(dense_t[:, :, :, :].rearrange("d t s g -> d t g s"),
                             b[0:ND, :].rearrange("d (t g s) -> d t g s", t=TILES, g=G))
                elif u < U1:
                    c = copy(cw[:, u - UW - 1, :], b[:, 0:PAIRS])
                else:
                    src, dst, rows = late[u - U1]
                    n = len(src)
                    if n > 1:
                        c = copy(dst, b[0:rows, 0:n * P].rearrange("r (n h) -> r n h", n=n))
                    else:
                        c = copy(dst, b[0:rows, 0:P])
                c.then_inc(prep_out[parity], 1)

        block = ctx.enter_context(nc.Block())

        @block.sync
        def _(sp):
            sp.dma_start(ids_sb[:, :, :], ids.rearrange("(t p) f -> p t f", p=P)).then_inc(ids_loaded, 16)
            sp.dma_start(w1raw[:, :, :], W1).then_inc(w1_loaded, 16)
            sp.dma_start(w1s[:, ONE:ONE + 1], b1.rearrange("(p o) -> p o", o=1)).then_inc(w1_loaded, 16)
            sp.dma_start(at(w2raw, 0, (1, H * F)), W2.rearrange("h i c -> h (i c)")).then_inc(w2_loaded, 16)
            sp.dma_start(dense_sb[:, :, :], dense.rearrange("(t p) d -> p t d", p=P)).then_inc(dense_loaded, 16)
            sp.dma_start(wt1[:, :, :], W_top1[0:2 * H, :].rearrange("(c p) n -> p c n", p=P)).then_inc(tower_loaded, 16)
            sp.dma_start(wt1d[:, :], W_top1[2 * H:2 * H + ND, :]).then_inc(tower_loaded, 16)
            sp.dma_start(wt2[:, :, :], W_top2.rearrange("(p m) n -> p m n", m=M1)).then_inc(tower_loaded, 16)
            sp.dma_start(wt3[:, :], W_top3.rearrange("(p m) o -> p (m o)", m=M2)).then_inc(tower_loaded, 16)
            sp.dma_start(bt1[:, :], b_top1.rearrange("(p m) -> p m", m=M1)).then_inc(tower_loaded, 16)
            sp.dma_start(bt2[:, :], b_top2.rearrange("(p m) -> p m", m=M2)).then_inc(tower_loaded, 16)
            sp.dma_start(b2s[:, 0:1], b2.rearrange("(p o) -> p o", o=1)).then_inc(tower_loaded, 16)
            sp.wait_ge(tile_out, TILES)
            sp.dma_start(out.rearrange("(a n) o -> a (n o)", a=1),
                         ys[:, :, :, :].rearrange("a t g s -> a (t g s)")).then_inc(stored, 16)
            sp.wait_ge(stored, 16)

        @block.gpsimd
        def _(pool):
            nc.gpsimd.memset(ident[:, :], 0.0).then_inc(ident_zero, 1)
            pool.wait_ge(ident_zero, 1)
            nc.gpsimd.affine_select(out=ident[:, :], in_=ident[:, :], compare_op=ALU.not_equal, fill=1.0,
                                    base=0, pattern=[[-1, P]], channel_multiplier=1).then_inc(ident_ready, 1)
            pool.wait_ge(ids_loaded, 16)
            for t in range(TILES):
                for f in range(F):
                    if t >= 2 and f == 0:
                        pool.wait_ge(x_transposed, 2 * (t - 2) + 1)
                    if t >= 2 and f == NAB:
                        pool.wait_ge(x_transposed, 2 * (t - 2) + 2)
                    done = ab_gathered[t % 2] if f < NAB else c_gathered[t % 2]
                    pool.indirect_dma_start(gathered[:, t % 2, f, :], None, tables[f],
                                            bass.IndirectOffsetOnAxis(ids_sb[:, t, f:f + 1], axis=0)
                                            ).then_inc(done, 16)

        @block.tensor
        def _(pe):
            pe.wait_ge(ident_ready, 1)
            pe.wait_ge(w2_loaded, 16)
            for u in range(UW):
                for c in range(WT * u, min(WT * u + WT, F)):
                    last = nc.tensor.transpose(bank[u][:, (c - WT * u) * P:(c - WT * u + 1) * P],
                                               at(w2raw, c, (F, H)), ident[:, :])
                last.then_inc(prep_filled, 1)
            pe.wait_ge(dense_loaded, 16)
            for t in range(TILES):
                last = nc.tensor.transpose(bank[UW][0:ND, t * P:(t + 1) * P], dense_sb[:, t, :], ident[:, :])
            last.then_inc(prep_filled, 1)
            pe.wait_ge(w1_ready, 1)
            for c in range(F):
                u = UW + 1 + c
                emptied(pe, c // WT)
                emptied(pe, u - 8)
                nc.tensor.matmul(prep_bank(u)[:, 0:PAIRS], at(w2t, c * P, (1, P)), w1s[:, :],
                                 start=True, stop=True).then_inc(prep_filled, 1)
            emptied(pe, U1 - 2)
            emptied(pe, U1 - 1)

            def moments(t):
                d, px, py = xdiag[t % 2], prodx[t % 2], prody[t % 2]
                pe.wait_ge(diag_ready, t + 1)
                pe.wait_ge(prod_ready, t + 1)
                for s in range(Q):
                    if s % XG == 0:
                        nx = XU * t + s // XG
                        if nx >= 3:
                            pe.wait_ge(x_out, nx - 2)
                    if s % YG == 0:
                        ny = YU * t + s // YG
                        if ny >= 2:
                            pe.wait_ge(y_out, ny - 1)
                    mx = nc.tensor.matmul(bank[nx % 3][0:XR, (s % XG) * NX:(s % XG + 1) * NX],
                                          at(px, s, (Q, XR)), at(d, s, (J * Q, G), (Q, J)),
                                          start=True, stop=True)
                    if s % XG == XG - 1:
                        mx.then_inc(x_filled, 1)
                    my = nc.tensor.matmul(bank[3 + ny % 2][0:YR, (s % YG) * NY:(s % YG + 1) * NY],
                                          at(py, s, (Q, YR)), at(d, NAB * Q + s, (J * Q, G), (Q, JY)),
                                          start=True, stop=True)
                    if s % YG == YG - 1:
                        my.then_inc(y_filled, 1)

            def layers(t):
                pe.wait_ge(x_out, XU * (t + 1))
                pe.wait_ge(y_out, YU * (t + 1))
                if t:
                    pe.wait_ge(tile_out, t)
                z = bank[ZB]
                terms = [(zwx[0:XR, :], tx[0:XR, F, :]), (zwab[0:AB, :], ty[0:AB, NC, :])]
                terms += [(zwp[0:YR, c, :], ty[0:YR, c, :]) for c in range(NC)]
                for n, (w, m) in enumerate(terms):
                    nc.tensor.matmul(z[:, 0:P], w, m, start=(n == 0), stop=(n == len(terms) - 1))
                terms = [(cx[0:XR, j, :], tx[0:XR, j, :]) for j in range(F)]
                terms += [(cy[0:AB, c, :], ty[0:AB, c, :]) for c in range(NC)]
                for n, (w, m) in enumerate(terms):
                    last = nc.tensor.matmul(z[:, P:2 * P], w, m, start=(n == 0), stop=(n == len(terms) - 1))
                last.then_inc(z_done, 1)

                if t == 0:
                    pe.wait_ge(tower_loaded, 16 * 7)
                pe.wait_ge(z_out, t + 1)
                if t:
                    pe.wait_ge(h2_act, t)
                    pe.wait_ge(h2_dve, t)
                for m in range(M1):
                    h = bank[H1A if m < M1 // 2 else H1B][:, (m % 2) * P:(m % 2 + 1) * P]
                    for c in range(2):
                        nc.tensor.matmul(h, at(wt1, c * N1 + m, (M1, P)), zs[:, c, :], start=(c == 0), stop=False)
                    last = nc.tensor.matmul(h, at(wt1d, m, (M1, P), rows=ND),
                                            dense_t[:, t, :, :].rearrange("d s g -> d (s g)"),
                                            start=False, stop=True)
                    if m % 2:
                        last.then_inc(h1_done, 1)
                pe.wait_ge(h1_act, t + 1)
                pe.wait_ge(h1_dve, t + 1)
                for m in range(M2):
                    h = bank[H1A if m == 0 else H1B][:, 2 * P:3 * P]
                    for c in range(M1):
                        last = nc.tensor.matmul(h, at(wt2, c * N2 + m, (M2, P)), h1s[:, c, :],
                                                start=(c == 0), stop=(c == M1 - 1))
                    last.then_inc(h2_done, 1)
                pe.wait_ge(h2_act, t + 1)
                pe.wait_ge(h2_dve, t + 1)
                for c in range(M2):
                    last = nc.tensor.matmul(z[0:1, 2 * P:3 * P], wt3[:, c:c + 1], h2s[:, c, :],
                                            start=(c == 0), stop=(c == M2 - 1))
                last.then_inc(y_done, 1)

            for t in range(TILES):
                moments(t)
                if t == 0:
                    pe.wait_ge(orders_added, 4)
                    pe.wait_ge(w1p_ready, 1)
                    for v, (srcs, _, rows) in enumerate(late):
                        u = U1 + v
                        if v >= 3:
                            emptied(pe, u - 3)
                        for n, src in enumerate(srcs):
                            last = nc.tensor.transpose(prep_bank(u)[0:rows, n * P:(n + 1) * P], src, ident[:, :])
                        last.then_inc(prep_filled, 1)
                    emptied(pe, U - 2)
                    emptied(pe, U - 1)
                layers(t)

        @block.scalar
        def _(act):
            empty_prep(act, nc.scalar.copy, 0, 0, U1)
            for t in range(TILES):
                d, x = xdiag[t % 2], xk[:, t % 2, :, :]
                act.wait_ge(x_transposed, 2 * t + 1)
                if t >= 2:
                    act.wait_ge(y_filled, YU * (t - 1))
                elif t == 1:
                    act.wait_ge(diag1_ready, 1)
                else:
                    act.wait_ge(consts_ready, 1)
                for g in range(G):
                    nc.scalar.copy(d[g * Q:(g + 1) * Q, g, 0:NAB, :], x[g * Q:(g + 1) * Q, 0:NAB, :])
                nc.scalar.copy(prody[t % 2][:, AB:YR, :], x[:, 0:NAB, :])
                act.wait_ge(x_transposed, 2 * t + 2)
                for g in range(G):
                    last = nc.scalar.copy(d[g * Q:(g + 1) * Q, g, NAB:F, :], x[g * Q:(g + 1) * Q, NAB:F, :])
                last.then_inc(diag_ready, 1)
                for u in range(XU):
                    n = XU * t + u
                    act.wait_ge(x_filled, n + 1)
                    if t and u == 0:
                        act.wait_ge(z_done, t)
                    nc.scalar.copy(tx[0:XR, :, u * XG * G:(u + 1) * XG * G].rearrange("r j (s g) -> r s g j", s=XG),
                                   bank[n % 3][0:XR, 0:XG * NX].rearrange("r (s g j) -> r s g j", s=XG, g=G)
                                   ).then_inc(x_out, 1)
                if t == 0:
                    empty_prep(act, nc.scalar.copy, 0, U1, U)
                    act.wait_ge(b2_scaled, 1)
                act.wait_ge(z_done, t + 1)
                nc.scalar.copy(zs[:, 0, :], bank[ZB][:, 0:P])
                nc.scalar.activation(zs[:, 1, :], bank[ZB][:, P:2 * P], ACT.Identity,
                                     bias=b2s[:, 1:2]).then_inc(z_out, 1)
                act.wait_ge(h1_done, 2 * t + 1)
                for m in range(M1 // 2):
                    last = nc.scalar.activation(h1s[:, m, :], bank[H1A][:, m * P:(m + 1) * P], ACT.Relu,
                                                bias=bt1[:, m:m + 1])
                last.then_inc(h1_act, 1)
                act.wait_ge(h2_done, 2 * t + 1)
                nc.scalar.activation(h2s[:, 0, :], bank[H1A][:, 2 * P:3 * P], ACT.Relu,
                                     bias=bt2[:, 0:1]).then_inc(h2_act, 1)
                act.wait_ge(y_done, t + 1)
                nc.scalar.copy(ys[:, t, :, :], bank[ZB][0:1, 2 * P:3 * P].rearrange("a (s g) -> a g s", g=G)
                               ).then_inc(tile_out, 1)

        @block.vector
        def _(dve):
            dve.wait_ge(w1_loaded, 32)
            nc.vector.tensor_tensor(w1both[:, :, :], w1raw[:, :, :], w1raw[:, :, :].rearrange("h p q -> h q p"),
                                    ALU.add).then_inc(w1_step, 1)
            dve.wait_ge(w1_step, 1)
            nc.vector.tensor_copy(at(w1both, 0, (F + 1, F)), at(w1raw, 0, (F + 1, F))).then_inc(w1_step, 1)
            dve.wait_ge(w1_step, 2)
            for q in range(NA):
                nc.vector.tensor_copy(at(w1s, tri(q), (TA, 2), (1, q + 1)),
                                      at(w1both, q * F, (NA * (F + 1), 2), (1, q + 1)))
            for q in range(NC):
                nc.vector.tensor_copy(at(w1s, 2 * TA + tri(q), (1, q + 1)),
                                      at(w1both, (NAB + q) * F + NAB, (1, q + 1)))
            nc.vector.tensor_copy(at(w1s, CAB, (NA, NA), (1, NA)), at(w1both, NA, (F, NA), (1, NA)))
            nc.vector.tensor_copy(at(w1s, CPC, (NC, NAB), (1, NC)),
                                  at(w1both, NAB, (F, NAB), (1, NC))).then_inc(w1_ready, 1)
            nc.vector.memset(xdiag[0][:, :, :, :], 0.0).then_inc(w1_step, 1)
            dve.wait_ge(w1_step, 3)
            for g in range(G):
                nc.vector.memset(xdiag[0][g * Q:(g + 1) * Q, g, F, :], 1.0)
            nc.vector.memset(prodx[1][:, ONE, :], 1.0)
            nc.vector.memset(prodx[0][:, ONE, :], 1.0).then_inc(consts_ready, 1)
            nc.vector.memset(w1p[:, :, :], 0.0).then_inc(w1_step, 1)
            dve.wait_ge(w1_step, 4)
            nc.vector.tensor_copy(at(w1p, AB, (YR, NC), (1, NAB)),
                                  at(w1both, NAB, (1, NC), (F, NAB))).then_inc(w1p_ready, 1)
            dve.wait_ge(tower_loaded, 16 * 7)
            nc.vector.tensor_scalar(b2s[:, 1:2], b2s[:, 0:1], float(E), None, ALU.mult).then_inc(b2_scaled, 1)
            empty_prep(dve, nc.vector.tensor_copy, 1, 0, U1)
            dve.wait_ge(prep_filled, U1)
            nc.vector.memset(xdiag[1][:, :, :, :], 0.0).then_inc(w1_step, 1)
            dve.wait_ge(w1_step, 5)
            for g in range(G):
                last = nc.vector.memset(xdiag[1][g * Q:(g + 1) * Q, g, F, :], 1.0)
            last.then_inc(diag1_ready, 1)

            def add_orders(step):
                second = step % 2
                if step == 0:
                    emptied(dve, U1 - 2)
                    emptied(dve, U1 - 1)
                if step == 2:
                    dve.wait_ge(orders_added, 2)

                def add(dst, src, dims_dst, dims_src):
                    d = at(cw, dst, *dims_dst)
                    return nc.vector.tensor_tensor(d, d, at(cw, src, *dims_src), ALU.add)

                other_q = step < 2
                for q in range(NA):
                    n = q + 1 if other_q else q
                    if not n:
                        continue
                    if not second:
                        pa = (q * PAIRS + CAB, (NA, n)) if other_q else (CAB + NA * q, (PAIRS, n))
                        add(NA * PAIRS + tri(q), pa[0], ((PAIRS, NA), (1, n)), ((1, NA), pa[1]))
                        pb = ((NA + q) * PAIRS + CAB, (1, n)) if other_q else (NA * PAIRS + CAB + q, (PAIRS, n))
                        last = add(TA + tri(q), pb[0], ((PAIRS, NA), (1, n)), ((NA, NA), pb[1]))
                    else:
                        off, st = (q * PAIRS + CPC, NC) if other_q else (CPC + NC * q, PAIRS)
                        last = add(NAB * PAIRS + tri(q), off, ((TA, 2), (PAIRS, NC), (1, n)),
                                   ((NA * PAIRS + NA * NC, 2), (1, NC), (st, n)))
                if second:
                    for q in range(NC):
                        n = q + 1 if other_q else q
                        if n:
                            off, st = (((NAB + q) * PAIRS + CPC, 1) if other_q else (NAB * PAIRS + CPC + q, PAIRS))
                            last = add(2 * TA + tri(q), off, ((PAIRS, NAB), (1, n)), ((NC, NAB), (st, n)))
                else:
                    if other_q:
                        last = add(NAB * PAIRS + CAB, NA * PAIRS + CPC, ((NA, NA), (1, NA), (PAIRS, NC)),
                                   ((NC, NA), (PAIRS, NA), (1, NC)))
                    else:
                        last = add(NAB * PAIRS + CAB, CPC + NA * NC, ((NA, NA), (1, NA), (PAIRS, NC)),
                                   ((PAIRS, NA), (NC, NA), (1, NC)))
                last.then_inc(orders_added, 1)

            def products(t):
                b = t % 2
                x, px, py = xk, prodx[b], prody[b]
                x0 = b * F * Q
                dve.wait_ge(ab_gathered[b], 16 * NAB * (t // 2 + 1))
                if t >= 2:
                    dve.wait_ge(diag_ready, t - 1)
                nc.vector.transpose(at(x, x0, (1, NAB * Q)), at(gathered, x0, (1, NAB * Q))
                                    ).then_inc(x_transposed, 1)
                dve.wait_ge(x_transposed, 2 * t + 1)
                if t >= 2:
                    dve.wait_ge(y_filled, YU * (t - 1))
                for q in range(NA):
                    nc.vector.tensor_tensor(at(px, tri(q) * Q, (TA * Q, 2), (Q, q + 1), (1, Q)),
                                            at(x, x0, (NA * Q, 2), (Q, q + 1), (1, Q)),
                                            at(x, x0 + q * Q, (NA * Q, 2), (0, q + 1), (1, Q)), ALU.mult)
                nc.vector.tensor_tensor(at(py, 0, (NA * Q, NA), (Q, NA), (1, Q)),
                                        at(x, x0, (Q, NA), (0, NA), (1, Q)),
                                        at(x, x0 + NA * Q, (0, NA), (Q, NA), (1, Q)), ALU.mult)
                xc = x0 + NAB * Q
                dve.wait_ge(c_gathered[b], 16 * NC * (t // 2 + 1))
                nc.vector.transpose(at(x, xc, (1, NC * Q)), at(gathered, xc, (1, NC * Q))
                                    ).then_inc(x_transposed, 1)
                dve.wait_ge(x_transposed, 2 * t + 2)
                for q in range(NC):
                    last = nc.vector.tensor_tensor(at(px, (2 * TA + tri(q)) * Q, (Q, q + 1), (1, Q)),
                                                   at(x, xc, (Q, q + 1), (1, Q)),
                                                   at(x, xc + q * Q, (0, q + 1), (1, Q)), ALU.mult)
                last.then_inc(prod_ready, 1)

            for t in range(TILES):
                products(t)
                for u in range(YU):
                    if t == 0:
                        add_orders(u)
                    n = YU * t + u
                    dve.wait_ge(y_filled, n + 1)
                    if t and u == 0:
                        dve.wait_ge(z_done, t)
                    nc.vector.tensor_copy(
                        ty[0:YR, :, u * YG * G:(u + 1) * YG * G].rearrange("r j (s g) -> r s g j", s=YG),
                        bank[3 + n % 2][0:YR, 0:YG * NY].rearrange("r (s g j) -> r s g j", s=YG, g=G)
                    ).then_inc(y_out, 1)
                if t == 0:
                    empty_prep(dve, nc.vector.tensor_copy, 1, U1, U)
                dve.wait_ge(h1_done, 2 * t + 2)
                for m in range(M1 // 2, M1):
                    last = nc.vector.tensor_scalar(h1s[:, m, :], bank[H1B][:, (m % 2) * P:(m % 2 + 1) * P],
                                                   bt1[:, m:m + 1], 0.0, ALU.add, ALU.max)
                last.then_inc(h1_dve, 1)
                dve.wait_ge(h2_done, 2 * t + 2)
                nc.vector.tensor_scalar(h2s[:, 1, :], bank[H1B][:, 2 * P:3 * P], bt2[:, 1:2], 0.0,
                                        ALU.add, ALU.max).then_inc(h2_dve, 1)


_INS = (["dense_ctx", "ids"] + [f"tbl_{f}" for f in range(26)] +
        ["W_top1", "b_top1", "W_top2", "b_top2", "W_top3", "L0_rec_W1", "L0_rec_b1", "L0_rec_W2", "L0_rec_b2"])


def kernel(**inputs):
    import numpy as _np
    import concourse.bacc as _bacc
    from concourse import mybir as _mybir
    from concourse.bass_utils import run_bass_kernel_spmd as _run

    nc = _bacc.Bacc("TRN2", target_bir_lowering=False, num_devices=1)
    arrays, aps = {}, {}
    for name in _INS:
        a = _np.ascontiguousarray(inputs[name])
        arrays[f"in_{name}"] = a
        aps[name] = nc.dram_tensor(f"in_{name}", a.shape, _mybir.dt.from_np(a.dtype), kind="ExternalInput").ap()
    out = nc.dram_tensor("out_y", (inputs["ids"].shape[0], 1), _mybir.dt.float32, kind="ExternalOutput").ap()
    build(nc, aps["dense_ctx"], aps["ids"], [aps[f"tbl_{f}"] for f in range(26)], aps["W_top1"], aps["b_top1"],
          aps["W_top2"], aps["b_top2"], aps["W_top3"], aps["L0_rec_W1"], aps["L0_rec_b1"], aps["L0_rec_W2"],
          aps["L0_rec_b2"], out)
    r = _run(nc, [arrays], core_ids=[0])
    return r.results[0]["out_y"]
```

```python
from contextlib import ExitStack

import concourse.bass as bass
from concourse import mybir

ACT = mybir.ActivationFunctionType
ALU = mybir.AluOpType
F32 = mybir.dt.float32
I32 = mybir.dt.int32

P = 128
Q = 32
G = P // Q


def build(nc, dense, ids, tables, W_top1, b_top1, W_top2, b_top2, W_top3, W1, b1, W2, b2, out):
    BATCH, F = ids.shape
    E = tables[0].shape[1]
    H = W1.shape[0]
    ND = dense.shape[0]
    N1, N2 = W_top1.shape[1], W_top2.shape[1]
    M1, M2 = N1 // P, N2 // P
    TILES = BATCH // P
    assert E == Q and H == P and F == 26 and W_top1.shape[0] == 2 * H + ND

    NA, NC = 9, 8
    NAB = 2 * NA
    assert NAB + NC == F

    def tri(n):
        return n * (n + 1) // 2

    TA = tri(NA)
    XR = 2 * TA + tri(NC) + 1
    ONE = XR - 1
    AB = NA * NA
    YR = AB + NAB
    CAB = XR
    CPC = CAB + AB
    PAIRS = CPC + NAB * NC
    J = F + 1
    JY = NC + 1
    JXS, JYS = 32, 25
    NX, NY = G * JXS, G * JYS
    XG, YG = 4, 4
    XU, YU = Q // XG, Q // YG
    WARM = 14
    U1 = F

    with ExitStack() as ctx:
        def sb(name, shape, dt=F32):
            return ctx.enter_context(nc.sbuf_tensor(name, shape, dt))

        def sem(name):
            return ctx.enter_context(nc.semaphore(name))

        bank = [ctx.enter_context(nc.psum_tensor(f"bank{i}", [P, 512], F32)) for i in range(8)]
        ZB, H1A, H1B = 5, 6, 7
        LAST1, LAST2, LAST3 = (6, 7, 0, 1), (3, 4), 2

        ident = sb("ident", [P, P])
        ids_sb = sb("ids_sb", [P, TILES, F], I32)
        gathered = sb("gathered", [P, 2, F, E])
        xk = sb("xk", [P, 2, F, Q])
        DW = (G - 1) * J + JXS
        xdiag = [sb(f"xdiag{i}", [P, DW, Q]) for i in range(2)]
        prodx = [sb(f"prodx{i}", [P, XR, Q]) for i in range(2)]
        prody = [sb(f"prody{i}", [P, YR, Q]) for i in range(2)]
        tx = sb("tx", [P, J, P])
        ty = sb("ty", [P, JY, P])
        w1raw = sb("w1raw", [P, F, F])
        w1both = sb("w1both", [P, F, F])
        w1s = sb("w1s", [P, PAIRS])
        w1sb = sb("w1sb", [P, PAIRS])
        cw = sb("cw", [P, F, PAIRS])
        w1p = sb("w1p", [P, NC, YR])
        cx = sb("cx", [P, F, P])
        cy = sb("cy", [P, NC, P])
        zwx = sb("zwx", [P, P])
        zwab = sb("zwab", [P, P])
        zwp = sb("zwp", [P, NC, P])
        wt1 = sb("wt1", [P, 2, N1])
        wt1d = sb("wt1d", [ND, N1])
        wt2 = sb("wt2", [P, M1, N2])
        wt3 = sb("wt3", [P, M2])
        bt1 = sb("bt1", [P, M1])
        bt2 = sb("bt2", [P, M2])
        b2s = sb("b2s", [P, 2])
        dense_t = sb("dense_t", [ND, TILES, P])
        zs = sb("zs", [P, 2, P])
        h1s = sb("h1s", [P, M1, P])
        h2s = sb("h2s", [P, M2, P])
        ys = sb("ys", [1, TILES, G, Q])

        w2t = tx

        def at(t, off, *dims, rows=P, row0=0):
            width = 1
            for n in t.shape[1:]:
                width *= n
            return bass.AP(t, row0 * width + off, [[width, rows]] + [list(d) for d in dims])

        ids_loaded = sem("ids_loaded")
        w1_loaded = sem("w1_loaded")
        w2_loaded = [sem(f"w2_loaded{i}") for i in range(2)]
        dense_loaded = sem("dense_loaded")
        tower_loaded = sem("tower_loaded")
        ident_zero = sem("ident_zero")
        ident_ready = sem("ident_ready")
        gathered_in = [[sem(f"gathered_{blk}{i}") for i in range(2)] for blk in "abc"]
        x_transposed = sem("x_transposed")
        w1_step = sem("w1_step")
        w1_ready = sem("w1_ready")
        w1p_ready = sem("w1p_ready")
        b2_scaled = sem("b2_scaled")
        zeroed = sem("zeroed")
        consts_ready = sem("consts_ready")
        prep_filled = sem("prep_filled")
        prep_out = sem("prep_out")
        orders_added = sem("orders_added")
        diag_ready = sem("diag_ready")
        prod_ready = sem("prod_ready")
        x_filled = sem("x_filled")
        y_filled = sem("y_filled")
        x_out = sem("x_out")
        y_out = sem("y_out")
        z_done = sem("z_done")
        z_out = sem("z_out")
        h1_done = sem("h1_done")
        h1_act = sem("h1_act")
        h1_dve = sem("h1_dve")
        h2_done = sem("h2_done")
        h2_act = sem("h2_act")
        h2_dve = sem("h2_dve")
        y_done = sem("y_done")
        tile_out = sem("tile_out")
        stored = sem("stored")

        late = [([w1s[:, 0:XR]], zwx[0:XR, :], XR), ([w1s[:, CAB:CAB + AB]], zwab[0:AB, :], AB)]
        for j0 in range(0, NC, 4):
            late.append(([w1p[:, j0 + i, :] for i in range(4)], zwp[0:YR, j0:j0 + 4, :], YR))
        W1_ONLY = len(late)
        for j0 in range(0, F, 4):
            n = min(4, F - j0)
            late.append(([at(cw, (j0 + i) * PAIRS, (1, XR)) for i in range(n)], cx[0:XR, j0:j0 + n, :], XR))
        for j0 in range(0, NC, 4):
            late.append(([at(cw, (NAB + j0 + i) * PAIRS + CAB, (1, AB)) for i in range(4)],
                         cy[0:AB, j0:j0 + 4, :], AB))
        U = U1 + len(late)

        def prep_bank(u):
            return bank[u % 8] if u < U1 else bank[5 + (u - U1) % 3]

        def emptied(eng, u):
            eng.wait_ge(prep_out, u + 1)

        def empty_prep(act, lo, hi):
            for u in range(lo, hi):
                b = prep_bank(u)
                act.wait_ge(prep_filled, u + 1)
                if u < U1:
                    c = nc.scalar.copy(cw[:, u, :], b[:, 0:PAIRS])
                else:
                    src, dst, rows = late[u - U1]
                    n = len(src)
                    if n > 1:
                        c = nc.scalar.copy(dst, b[0:rows, 0:n * P].rearrange("r (n h) -> r n h", n=n))
                    else:
                        c = nc.scalar.copy(dst, b[0:rows, 0:P])
                c.then_inc(prep_out, 1)

        BLOCKS = ((0, NA), (NA, NA), (NAB, NC))

        block = ctx.enter_context(nc.Block())

        @block.sync
        def _(sp):
            sp.dma_start(ids_sb[:, :, :], ids.rearrange("(t p) f -> p t f", p=P)).then_inc(ids_loaded, 16)
            sp.dma_start(w1raw[:, :, :], W1).then_inc(w1_loaded, 16)
            sp.dma_start(w1s[:, ONE:ONE + 1], b1.rearrange("(p o) -> p o", o=1)).then_inc(w1_loaded, 16)
            for n, c in enumerate((slice(0, NA), slice(NA, F))):
                sp.dma_start(w2t[:, c, :], W2[:, c, :]).then_inc(w2_loaded[n], 16)
            sp.dma_start(dense_t[:, :, :], dense).then_inc(dense_loaded, 16)
            sp.dma_start(wt1[:, :, :], W_top1[0:2 * H, :].rearrange("(c p) n -> p c n", p=P)).then_inc(tower_loaded, 16)
            sp.dma_start(wt1d[:, :], W_top1[2 * H:2 * H + ND, :]).then_inc(tower_loaded, 16)
            sp.dma_start(wt2[:, :, :], W_top2.rearrange("(p m) n -> p m n", m=M1)).then_inc(tower_loaded, 16)
            sp.dma_start(wt3[:, :], W_top3.rearrange("(p m) o -> p (m o)", m=M2)).then_inc(tower_loaded, 16)
            sp.dma_start(bt1[:, :], b_top1.rearrange("(p m) -> p m", m=M1)).then_inc(tower_loaded, 16)
            sp.dma_start(bt2[:, :], b_top2.rearrange("(p m) -> p m", m=M2)).then_inc(tower_loaded, 16)
            sp.dma_start(b2s[:, 0:1], b2.rearrange("(p o) -> p o", o=1)).then_inc(tower_loaded, 16)
            sp.wait_ge(tile_out, TILES)
            sp.dma_start(out.rearrange("(a n) o -> a (n o)", a=1),
                         ys[:, :, :, :].rearrange("a t g s -> a (t g s)")).then_inc(stored, 16)
            sp.wait_ge(stored, 16)

        @block.gpsimd
        def _(pool):
            nc.gpsimd.memset(ident[:, :], 0.0).then_inc(ident_zero, 1)
            pool.wait_ge(ident_zero, 1)
            nc.gpsimd.affine_select(out=ident[:, :], in_=ident[:, :], compare_op=ALU.not_equal, fill=1.0,
                                    base=0, pattern=[[-1, P]], channel_multiplier=1).then_inc(ident_ready, 1)
            pool.wait_ge(ids_loaded, 16)
            for t in range(TILES):
                for n, (f0, fields) in enumerate(BLOCKS):
                    if t >= 2:
                        pool.wait_ge(x_transposed, 3 * (t - 2) + n + 1)
                    for f in range(f0, f0 + fields):
                        pool.indirect_dma_start(gathered[:, t % 2, f, :], None, tables[f],
                                                bass.IndirectOffsetOnAxis(ids_sb[:, t, f:f + 1], axis=0)
                                                ).then_inc(gathered_in[n][t % 2], 16)

        @block.tensor
        def _(pe):
            def weight_transposes(lo, hi):
                for v in range(lo, hi):
                    srcs, _, rows = late[v]
                    u = U1 + v
                    if v >= 3:
                        emptied(pe, u - 3)
                    for n, src in enumerate(srcs):
                        last = nc.tensor.transpose(prep_bank(u)[0:rows, n * P:(n + 1) * P], src, ident[:, :])
                    last.then_inc(prep_filled, 1)

            pe.wait_ge(ident_ready, 1)
            for _ in range(WARM):
                nc.tensor.matmul(bank[7][:, 0:P], ident[:, :], ident[:, :], start=True, stop=True)
            pe.wait_ge(w1_ready, 1)
            for c in range(F):
                if c in (0, NA):
                    pe.wait_ge(w2_loaded[c // NA], 16)
                if c >= 8:
                    emptied(pe, c - 8)
                if c == NA:
                    pe.wait_ge(w1_ready, 2)
                nc.tensor.matmul(prep_bank(c)[:, 0:PAIRS], w2t[:, c, :], (w1sb if NA <= c < NAB else w1s)[:, :],
                                 start=True, stop=True).then_inc(prep_filled, 1)
            emptied(pe, U1 - 1)
            pe.wait_ge(w1p_ready, 1)
            weight_transposes(0, W1_ONLY)

            def moments(t, lo, hi):
                d, px, py = xdiag[t % 2], prodx[t % 2], prody[t % 2]
                pe.wait_ge(diag_ready, 3 * (t + 1))
                pe.wait_ge(prod_ready, 3 * (t + 1))
                for s in range(lo, hi):
                    if s % XG == 0:
                        nx = XU * t + s // XG
                        if nx >= 3:
                            pe.wait_ge(x_out, nx - 2)
                    if s % YG == 0:
                        ny = YU * t + s // YG
                        if ny >= 2:
                            pe.wait_ge(y_out, ny - 1)
                    mx = nc.tensor.matmul(bank[nx % 3][0:XR, (s % XG) * NX:(s % XG + 1) * NX],
                                          at(px, s, (Q, XR)), at(d, s, (J * Q, G), (Q, JXS)),
                                          start=True, stop=True)
                    if s % XG == XG - 1:
                        mx.then_inc(x_filled, 1)
                    my = nc.tensor.matmul(bank[3 + ny % 2][0:YR, (s % YG) * NY:(s % YG + 1) * NY],
                                          at(py, s, (Q, YR)), at(d, (J - JYS) * Q + s, (J * Q, G), (Q, JYS)),
                                          start=True, stop=True)
                    if s % YG == YG - 1:
                        my.then_inc(y_filled, 1)

            def cin(t):
                pe.wait_ge(x_out, XU * (t + 1))
                pe.wait_ge(y_out, YU * (t + 1))
                if t:
                    pe.wait_ge(z_out, 2 * t)
                    pe.wait_ge(h2_dve, t)
                z1, z2 = bank[H1B][:, 3 * P:4 * P], bank[ZB][:, 0:P]
                terms = [(zwx[0:XR, :], tx[0:XR, F, :]), (zwab[0:AB, :], ty[0:AB, NC, :])]
                terms += [(zwp[0:YR, c, :], ty[0:YR, c, :]) for c in range(NC)]
                for n, (w, m) in enumerate(terms):
                    last = nc.tensor.matmul(z1, w, m, start=(n == 0), stop=(n == len(terms) - 1))
                last.then_inc(z_done, 1)
                terms = [(cx[0:XR, j, :], tx[0:XR, j, :]) for j in range(F)]
                terms += [(cy[0:AB, c, :], ty[0:AB, c, :]) for c in range(NC)]
                for n, (w, m) in enumerate(terms):
                    last = nc.tensor.matmul(z2, w, m, start=(n == 0), stop=(n == len(terms) - 1))
                last.then_inc(z_done, 1)

            def tower1(t):
                if t == 0:
                    pe.wait_ge(tower_loaded, 16 * 7)
                    pe.wait_ge(dense_loaded, 16)
                pe.wait_ge(z_out, 2 * (t + 1))
                if t:
                    pe.wait_ge(tile_out, t)
                    pe.wait_ge(h2_dve, t)
                for m in range(M1):
                    h = bank[H1A if m < M1 // 2 else H1B][:, (m % 2) * P:(m % 2 + 1) * P]
                    for c in range(2):
                        nc.tensor.matmul(h, at(wt1, c * N1 + m, (M1, P)), zs[:, c, :], start=(c == 0), stop=False)
                    last = nc.tensor.matmul(h, at(wt1d, m, (M1, P), rows=ND),
                                            dense_t[:, t, :],
                                            start=False, stop=True)
                    if m % 2:
                        last.then_inc(h1_done, 1)

            def tower2(t):
                pe.wait_ge(h1_act, t + 1)
                pe.wait_ge(h1_dve, t + 1)
                for m in range(M2):
                    h = bank[H1A if m == 0 else H1B][:, 2 * P:3 * P]
                    for c in range(M1):
                        last = nc.tensor.matmul(h, at(wt2, c * N2 + m, (M2, P)), h1s[:, c, :],
                                                start=(c == 0), stop=(c == M1 - 1))
                    last.then_inc(h2_done, 1)

            def tower3(t):
                pe.wait_ge(h2_act, t + 1)
                pe.wait_ge(h2_dve, t + 1)
                for c in range(M2):
                    last = nc.tensor.matmul(bank[H1A][0:1, 3 * P:4 * P], wt3[:, c:c + 1], h2s[:, c, :],
                                            start=(c == 0), stop=(c == M2 - 1))
                last.then_inc(y_done, 1)

            pe.wait_ge(orders_added, 4)
            weight_transposes(W1_ONLY, U - U1 - 4)
            for n in range(4):
                moments(0, n * Q // 4, (n + 1) * Q // 4)
                weight_transposes(U - U1 - 4 + n, U - U1 - 3 + n)
            emptied(pe, U - 1)
            cin(0)
            for t in range(1, TILES):
                moments(t, 0, Q // 4)
                tower1(t - 1)
                moments(t, Q // 4, Q // 2)
                tower2(t - 1)
                moments(t, Q // 2, Q)
                tower3(t - 1)
                cin(t)
            t = TILES - 1
            pe.wait_ge(z_out, 2 * t + 1)
            pe.wait_ge(tile_out, t)
            for m in range(M1):
                h = bank[LAST1[m]][:, 0:P]
                nc.tensor.matmul(h, at(wt1d, m, (M1, P), rows=ND), dense_t[:, t, :], start=True, stop=False)
                nc.tensor.matmul(h, at(wt1, m, (M1, P)), zs[:, 0, :], start=False, stop=False)
            pe.wait_ge(z_out, 2 * t + 2)
            for m in range(M1):
                nc.tensor.matmul(bank[LAST1[m]][:, 0:P], at(wt1, N1 + m, (M1, P)), zs[:, 1, :],
                                 start=False, stop=True).then_inc(h1_done, 1)
            for c in range(M1):
                pe.wait_ge((h1_act, h1_dve)[c % 2], t + c // 2 + 1)
                for m in range(M2):
                    last = nc.tensor.matmul(bank[LAST2[m]][:, 0:P], at(wt2, c * N2 + m, (M2, P)), h1s[:, c, :],
                                            start=(c == 0), stop=(c == M1 - 1))
                    if c == M1 - 1:
                        last.then_inc(h2_done, 1)
            for c in range(M2):
                pe.wait_ge((h2_act, h2_dve)[c], t + 1)
                last = nc.tensor.matmul(bank[LAST3][0:1, 0:P], wt3[:, c:c + 1], h2s[:, c, :],
                                        start=(c == 0), stop=(c == M2 - 1))
            last.then_inc(y_done, 1)

        @block.scalar
        def _(act):
            def diagonal(t, n):
                d, x = xdiag[t % 2], xk[:, t % 2, :, :]
                f0, fields = BLOCKS[n]
                if t < 2 and n == 0:
                    act.wait_ge(consts_ready, t + 1)
                if t >= 2 and n == 0:
                    act.wait_ge(y_filled, YU * (t - 1))
                act.wait_ge(x_transposed, 3 * t + n + 1)
                if f0 < NAB:
                    nc.scalar.copy(prody[t % 2][:, AB + f0:AB + f0 + fields, :], x[:, f0:f0 + fields, :])
                for g in range(G):
                    last = nc.scalar.copy(d[g * Q:(g + 1) * Q, g * J + f0:g * J + f0 + fields, :],
                                          x[g * Q:(g + 1) * Q, f0:f0 + fields, :])
                last.then_inc(diag_ready, 1)

            def sums(t, lo, hi):
                for u in range(lo, hi):
                    n = XU * t + u
                    act.wait_ge(x_filled, n + 1)
                    if t and u == 0:
                        act.wait_ge(z_done, 2 * t)
                    nc.scalar.copy(
                        tx[0:XR, :, u * XG * G:(u + 1) * XG * G].rearrange("r j (s g) -> r s g j", s=XG),
                        bank[n % 3][0:XR, :].rearrange("r (s g j) -> r s g j", s=XG, g=G)[:, :, :, 0:J]
                    ).then_inc(x_out, 1)
                    act.wait_ge(y_filled, n + 1)
                    nc.scalar.copy(
                        ty[0:YR, :, u * YG * G:(u + 1) * YG * G].rearrange("r j (s g) -> r s g j", s=YG),
                        bank[3 + n % 2][0:YR, 0:YG * NY].rearrange("r (s g j) -> r s g j", s=YG, g=G)
                        [:, :, :, JYS - JY:JYS]
                    ).then_inc(y_out, 1)

            def z_rows(t):
                if t == 0:
                    act.wait_ge(b2_scaled, 1)
                act.wait_ge(z_done, 2 * t + 1)
                nc.scalar.copy(zs[:, 0, :], bank[H1B][:, 3 * P:4 * P]).then_inc(z_out, 1)
                act.wait_ge(z_done, 2 * t + 2)
                nc.scalar.activation(zs[:, 1, :], bank[ZB][:, 0:P], ACT.Identity,
                                     bias=b2s[:, 1:2]).then_inc(z_out, 1)

            def hidden1(t):
                act.wait_ge(h1_done, 2 * t + 1)
                for m in range(M1 // 2):
                    last = nc.scalar.activation(h1s[:, m, :], bank[H1A][:, m * P:(m + 1) * P], ACT.Relu,
                                                bias=bt1[:, m:m + 1])
                last.then_inc(h1_act, 1)

            def hidden2(t):
                act.wait_ge(h2_done, 2 * t + 1)
                nc.scalar.activation(h2s[:, 0, :], bank[H1A][:, 2 * P:3 * P], ACT.Relu,
                                     bias=bt2[:, 0:1]).then_inc(h2_act, 1)

            def result(t, src):
                act.wait_ge(y_done, t + 1)
                nc.scalar.copy(ys[:, t, :, :], src.rearrange("a (s g) -> a g s", g=G)
                               ).then_inc(tile_out, 1)

            empty_prep(act, 0, U1 + W1_ONLY)
            diagonal(0, 0)
            diagonal(0, 1)
            empty_prep(act, U1 + W1_ONLY, U - 4)
            diagonal(0, 2)
            for n in range(4):
                sums(0, n * XU // 4, (n + 1) * XU // 4)
                empty_prep(act, U - 4 + n, U - 3 + n)
            for t in range(1, TILES):
                for n in range(len(BLOCKS)):
                    diagonal(t, n)
                z_rows(t - 1)
                sums(t, 0, XU // 4)
                hidden1(t - 1)
                sums(t, XU // 4, XU // 2)
                hidden2(t - 1)
                sums(t, XU // 2, XU)
                result(t - 1, bank[H1A][0:1, 3 * P:4 * P])
            t = TILES - 1
            z_rows(t)
            for m in range(0, M1, 2):
                act.wait_ge(h1_done, 2 * t + m + 1)
                nc.scalar.activation(h1s[:, m, :], bank[LAST1[m]][:, 0:P], ACT.Relu,
                                     bias=bt1[:, m:m + 1]).then_inc(h1_act, 1)
            act.wait_ge(h2_done, 2 * t + 1)
            nc.scalar.activation(h2s[:, 0, :], bank[LAST2[0]][:, 0:P], ACT.Relu,
                                 bias=bt2[:, 0:1]).then_inc(h2_act, 1)
            result(t, bank[LAST3][0:1, 0:P])

        @block.vector
        def _(dve):
            def constants(i):
                nc.vector.memset(xdiag[i][:, :, :], 0.0).then_inc(zeroed, 1)
                nc.vector.memset(prodx[i][:, ONE, :], 1.0)
                dve.wait_ge(zeroed, i + 1)
                for g in range(G):
                    last = nc.vector.memset(xdiag[i][g * Q:(g + 1) * Q, g * J + F, :], 1.0)
                last.then_inc(consts_ready, 1)

            constants(0)
            dve.wait_ge(w1_loaded, 32)
            nc.vector.tensor_tensor(w1both[:, :, :], w1raw[:, :, :], w1raw[:, :, :].rearrange("h p q -> h q p"),
                                    ALU.add).then_inc(w1_step, 1)
            dve.wait_ge(w1_step, 1)
            nc.vector.tensor_copy(at(w1both, 0, (F + 1, F)), at(w1raw, 0, (F + 1, F))).then_inc(w1_step, 1)
            dve.wait_ge(w1_step, 2)
            for q in range(NA):
                nc.vector.tensor_copy(at(w1s, tri(q), (TA, 2), (1, q + 1)),
                                      at(w1both, q * F, (NA * (F + 1), 2), (1, q + 1)))
            for q in range(NC):
                nc.vector.tensor_copy(at(w1s, 2 * TA + tri(q), (1, q + 1)),
                                      at(w1both, (NAB + q) * F + NAB, (1, q + 1)))
            nc.vector.tensor_copy(at(w1s, CAB, (NA, NA), (1, NA)), at(w1both, NA, (F, NA), (1, NA)))
            nc.vector.tensor_copy(at(w1s, CPC, (NC, NAB), (1, NC)),
                                  at(w1both, NAB, (F, NAB), (1, NC))).then_inc(w1_ready, 1)
            dve.wait_ge(w1_ready, 1)
            nc.vector.tensor_copy(w1sb[:, :], w1s[:, :]).then_inc(w1_step, 1)
            dve.wait_ge(w1_step, 3)
            nc.vector.tensor_copy(at(w1sb, CAB, (NA, NA), (1, NA)),
                                  at(w1both, NA * F, (F, NA), (1, NA))).then_inc(w1_ready, 1)
            nc.vector.memset(w1p[:, :, :], 0.0).then_inc(w1_step, 1)
            dve.wait_ge(w1_step, 4)
            nc.vector.tensor_copy(at(w1p, AB, (YR, NC), (1, NAB)),
                                  at(w1both, NAB, (1, NC), (F, NAB))).then_inc(w1p_ready, 1)
            dve.wait_ge(tower_loaded, 16 * 7)
            nc.vector.tensor_scalar(b2s[:, 1:2], b2s[:, 0:1], float(E), None, ALU.mult).then_inc(b2_scaled, 1)

            def add_orders(step):
                second = step >= 2
                other_q = step % 2 == 0
                if other_q:
                    emptied(dve, F - 1 if second else NAB - 1)
                else:
                    dve.wait_ge(orders_added, step)

                def add(dst, src, dims_dst, dims_src):
                    d = at(cw, dst, *dims_dst)
                    return nc.vector.tensor_tensor(d, d, at(cw, src, *dims_src), ALU.add)

                for q in range(NA):
                    n = q + 1 if other_q else q
                    if not n:
                        continue
                    if not second:
                        off, st = (q * PAIRS + CAB, NA) if other_q else (CAB + NA * q, PAIRS)
                        last = add(NA * PAIRS + tri(q), off, ((TA - NA * PAIRS, 2), (PAIRS, NA), (1, n)),
                                   ((NA * PAIRS, 2), (1, NA), (st, n)))
                    else:
                        off, st = (q * PAIRS + CPC, NC) if other_q else (CPC + NC * q, PAIRS)
                        last = add(NAB * PAIRS + tri(q), off, ((TA, 2), (PAIRS, NC), (1, n)),
                                   ((NA * PAIRS + NA * NC, 2), (1, NC), (st, n)))
                if second:
                    for q in range(NC):
                        n = q + 1 if other_q else q
                        if n:
                            off, st = (((NAB + q) * PAIRS + CPC, 1) if other_q else (NAB * PAIRS + CPC + q, PAIRS))
                            last = add(2 * TA + tri(q), off, ((PAIRS, NAB), (1, n)), ((NC, NAB), (st, n)))
                    if other_q:
                        last = add(NAB * PAIRS + CAB, NA * PAIRS + CPC, ((NA, NA), (1, NA), (PAIRS, NC)),
                                   ((NC, NA), (PAIRS, NA), (1, NC)))
                    else:
                        last = add(NAB * PAIRS + CAB, CPC + NA * NC, ((NA, NA), (1, NA), (PAIRS, NC)),
                                   ((PAIRS, NA), (NC, NA), (1, NC)))
                last.then_inc(orders_added, 1)

            def transposed(t, n):
                b = t % 2
                f0, fields = BLOCKS[n]
                dve.wait_ge(gathered_in[n][b], 16 * fields * (t // 2 + 1))
                if t >= 2:
                    dve.wait_ge(diag_ready, 3 * (t - 2) + n + 1)
                x0 = (b * F + f0) * Q
                nc.vector.transpose(at(xk, x0, (1, fields * Q)), at(gathered, x0, (1, fields * Q))
                                    ).then_inc(x_transposed, 1)

            def products(t, n):
                b = t % 2
                f0, fields = BLOCKS[n]
                x0 = (b * F + f0) * Q
                dve.wait_ge(x_transposed, 3 * t + n + 1)
                if t >= 2:
                    dve.wait_ge(y_filled, YU * (t - 1))
                for q in range(fields):
                    last = nc.vector.tensor_tensor(at(prodx[b], (TA * n + tri(q)) * Q, (Q, q + 1), (1, Q)),
                                                   at(xk, x0, (Q, q + 1), (1, Q)),
                                                   at(xk, x0 + q * Q, (0, q + 1), (1, Q)), ALU.mult)
                if n == 1:
                    last = nc.vector.tensor_tensor(at(prody[b], 0, (NA * Q, NA), (Q, NA), (1, Q)),
                                                   at(xk, x0 - NA * Q, (Q, NA), (0, NA), (1, Q)),
                                                   at(xk, x0, (0, NA), (Q, NA), (1, Q)), ALU.mult)
                last.then_inc(prod_ready, 1)

            def hidden1(t):
                dve.wait_ge(h1_done, 2 * t + 2)
                for m in range(M1 // 2, M1):
                    last = nc.vector.tensor_scalar(h1s[:, m, :], bank[H1B][:, (m % 2) * P:(m % 2 + 1) * P],
                                                   bt1[:, m:m + 1], 0.0, ALU.add, ALU.max)
                last.then_inc(h1_dve, 1)

            def hidden2(t):
                dve.wait_ge(h2_done, 2 * t + 2)
                nc.vector.tensor_scalar(h2s[:, 1, :], bank[H1B][:, 2 * P:3 * P], bt2[:, 1:2], 0.0,
                                        ALU.add, ALU.max).then_inc(h2_dve, 1)

            transposed(0, 0)
            products(0, 0)
            add_orders(0)
            add_orders(1)
            add_orders(2)
            transposed(0, 1)
            add_orders(3)
            products(0, 1)
            transposed(0, 2)
            products(0, 2)
            constants(1)
            for t in range(1, TILES):
                for n in range(len(BLOCKS)):
                    transposed(t, n)
                    products(t, n)
                hidden1(t - 1)
                hidden2(t - 1)
            t = TILES - 1
            for m in range(1, M1, 2):
                dve.wait_ge(h1_done, 2 * t + m + 1)
                nc.vector.tensor_scalar(h1s[:, m, :], bank[LAST1[m]][:, 0:P], bt1[:, m:m + 1], 0.0,
                                        ALU.add, ALU.max).then_inc(h1_dve, 1)
            dve.wait_ge(h2_done, 2 * t + 2)
            nc.vector.tensor_scalar(h2s[:, 1, :], bank[LAST2[1]][:, 0:P], bt2[:, 1:2], 0.0,
                                    ALU.add, ALU.max).then_inc(h2_dve, 1)


_INS = (["dense_ctx", "ids"] + [f"tbl_{f}" for f in range(26)] +
        ["W_top1", "b_top1", "W_top2", "b_top2", "W_top3", "L0_rec_W1", "L0_rec_b1", "L0_rec_W2", "L0_rec_b2"])


def kernel(**inputs):
    import numpy as _np
    import concourse.bacc as _bacc
    from concourse import mybir as _mybir
    from concourse.bass_utils import run_bass_kernel_spmd as _run

    nc = _bacc.Bacc("TRN2", target_bir_lowering=False, num_devices=1)
    arrays, aps = {}, {}
    for name in _INS:
        a = _np.asarray(inputs[name])
        if name == "L0_rec_W2":
            a = a.transpose(1, 2, 0)
        if name == "dense_ctx":
            a = a.reshape(-1, 4, 32, a.shape[1]).transpose(3, 0, 2, 1).reshape(a.shape[1], -1, 128)
        a = _np.ascontiguousarray(a)
        arrays[f"in_{name}"] = a
        aps[name] = nc.dram_tensor(f"in_{name}", a.shape, _mybir.dt.from_np(a.dtype), kind="ExternalInput").ap()
    out = nc.dram_tensor("out_y", (inputs["ids"].shape[0], 1), _mybir.dt.float32, kind="ExternalOutput").ap()
    build(nc, aps["dense_ctx"], aps["ids"], [aps[f"tbl_{f}"] for f in range(26)], aps["W_top1"], aps["b_top1"],
          aps["W_top2"], aps["b_top2"], aps["W_top3"], aps["L0_rec_W1"], aps["L0_rec_b1"], aps["L0_rec_W2"],
          aps["L0_rec_b2"], out)
    r = _run(nc, [arrays], core_ids=[0])
    return r.results[0]["out_y"]
```

```python
from contextlib import ExitStack

import concourse.bass as bass
from concourse import mybir

ACT = mybir.ActivationFunctionType
ALU = mybir.AluOpType
F32 = mybir.dt.float32
I32 = mybir.dt.int32

P = 128
Q = 32
G = P // Q


def build(nc, dense, ids, tables, W_top1, b_top1, W_top2, b_top2, W_top3, W1, b1, W2, b2, out):
    BATCH, F = ids.shape
    E = tables[0].shape[1]
    H = W1.shape[0]
    ND = dense.shape[0]
    N1, N2 = W_top1.shape[1], W_top2.shape[1]
    M1, M2 = N1 // P, N2 // P
    TILES = BATCH // P
    assert E == Q and H == P and F == 26 and W_top1.shape[0] == 2 * H + ND

    NA, NC = 9, 8
    NAB = 2 * NA
    assert NAB + NC == F

    def tri(n):
        return n * (n + 1) // 2

    TA = tri(NA)
    XR = 2 * TA + tri(NC) + 1
    ONE = XR - 1
    AB = NA * NA
    AC = NA * NC
    CAB = XR
    CPC = CAB + AB
    PAIRS = CPC + NAB * NC
    J = F + 1
    JY = NC + 1
    JXS, JYS = 32, 24
    NX, NY = G * JXS, G * JYS
    XG = YG = 4
    XU = YU = Q // XG
    WARM, WARM_HD, WARM_TILE = 14, 5, 13
    WARM_T = (0, 7, 2)
    PAIRS_AT = 16
    U1 = F

    with ExitStack() as ctx:
        def sb(name, shape, dt=F32):
            return ctx.enter_context(nc.sbuf_tensor(name, shape, dt))

        def sem(name):
            return ctx.enter_context(nc.semaphore(name))

        bank = [ctx.enter_context(nc.psum_tensor(f"bank{i}", [P, 512], F32)) for i in range(8)]
        Z1, ZP, Z2, H1A, H1B = 0, 1, 5, 6, 7
        LAST1, LAST2, LAST3 = (6, 7, 0, 1), (3, 4), 2

        ident = sb("ident", [P, P])
        ids_sb = sb("ids_sb", [P, TILES, F], I32)
        gathered = sb("gathered", [P, 2, F, E])
        xk = sb("xk", [P, 2, F, Q])
        DW = (G - 1) * J + JXS
        xdiag = [sb(f"xdiag{i}", [P, DW, Q]) for i in range(2)]
        prodx = [sb(f"prodx{i}", [P, XR, Q]) for i in range(2)]
        prody = [sb(f"prody{i}", [P, AB, Q]) for i in range(2)]
        tx = sb("tx", [P, J, P])
        ty = sb("ty", [P, JY, P])
        w1raw = sb("w1raw", [P, F, F])
        w1both = sb("w1both", [P, F, F])
        w1s = sb("w1s", [P, PAIRS])
        w1sb = sb("w1sb", [P, PAIRS])
        cw = sb("cw", [P, F, PAIRS])
        cx = sb("cx", [P, F, P])
        cy = sb("cy", [P, NC, P])
        zwx = sb("zwx", [P, P])
        zwab = sb("zwab", [P, P])
        zwc = sb("zwc", [P, 2, P])
        wt1 = sb("wt1", [P, 2, N1])
        wt1d = sb("wt1d", [ND, N1])
        wt2 = sb("wt2", [P, M1, N2])
        wt3 = sb("wt3", [P, M2])
        bt1 = sb("bt1", [P, M1])
        bt2 = sb("bt2", [P, M2])
        b2s = sb("b2s", [P, 2])
        PC = 3
        pair_prod = [sb(f"pair_prod{i}", [P, PC * NC, E]) for i in range(2)]
        STEPS = NAB // PC
        pair_sum = sb("pair_sum", [P, 2 * AC])
        pair_rows = sb("pair_rows", [P, 2, P])
        zs = sb("zs", [P, 2, P])
        h2s = sb("h2s", [P, M2, P])
        dense_t = sb("dense_t", [ND, TILES, P])
        hd = sb("hd", [P, M1, BATCH])

        w2t = tx

        def at(t, off, *dims, rows=P, row0=0):
            width = 1
            for n in t.shape[1:]:
                width *= n
            return bass.AP(t, row0 * width + off, [[width, rows]] + [list(d) for d in dims])

        h1sum = w1raw
        h1s = at(w1both, 0, (P, M1), (1, P))
        ys = at(dense_t, 0, (P, TILES), (Q, G), (1, Q), rows=1)

        ids_loaded = sem("ids_loaded")
        w1_loaded = sem("w1_loaded")
        w2_loaded = [sem(f"w2_loaded{i}") for i in range(2)]
        dense_loaded = sem("dense_loaded")
        tower_loaded = sem("tower_loaded")
        ident_zero = sem("ident_zero")
        ident_ready = sem("ident_ready")
        PARTS = ((0, NA, 0, 0), (NA, NA, NA, TA), (NAB, NC - 2, NAB, 2 * TA), (F - 2, 2, NAB, 2 * TA))
        NP = len(PARTS)
        gathered_in = [[sem(f"gathered_part{n}{i}") for i in range(2)] for n in range(NP)]
        x_transposed = sem("x_transposed")
        w1_step = sem("w1_step")
        w1_ready = sem("w1_ready")
        pair_multiplied = sem("pair_multiplied")
        pair_summed = sem("pair_summed")
        pair_filled = sem("pair_filled")
        pair_out = sem("pair_out")
        b2_scaled = sem("b2_scaled")
        zeroed = sem("zeroed")
        consts_ready = sem("consts_ready")
        prep_filled = sem("prep_filled")
        prep_out = sem("prep_out")
        orders_added = sem("orders_added")
        diag_ready = sem("diag_ready")
        prod_ready = sem("prod_ready")
        x_filled = sem("x_filled")
        y_filled = sem("y_filled")
        x_out = sem("x_out")
        y_out = sem("y_out")
        z_done = sem("z_done")
        z_out = sem("z_out")
        h1_done = sem("h1_done")
        hd_done = sem("hd_done")
        hd_out = sem("hd_out")
        h1_added = sem("h1_added")
        h1_act = sem("h1_act")
        h1_dve = sem("h1_dve")
        h2_done = sem("h2_done")
        h2_act = sem("h2_act")
        h2_dve = sem("h2_dve")
        y_done = sem("y_done")
        tile_out = sem("tile_out")
        stored = sem("stored")

        late = [([w1s[:, 0:XR]], zwx[0:XR, :], XR), ([w1s[:, CAB:CAB + AB]], zwab[0:AB, :], AB)]
        late.append(([w1s[:, CPC + i * AC:CPC + (i + 1) * AC] for i in range(2)], zwc[0:AC, :, :], AC))
        EARLY = len(late)
        for j0 in range(0, F, 4):
            n = min(4, F - j0)
            late.append(([at(cw, (j0 + i) * PAIRS, (1, XR)) for i in range(n)], cx[0:XR, j0:j0 + n, :], XR))
        for j0 in range(0, NC, 4):
            late.append(([at(cw, (NAB + j0 + i) * PAIRS + CAB, (1, AB)) for i in range(4)],
                         cy[0:AB, j0:j0 + 4, :], AB))
        U = U1 + len(late)
        LATE_PARTS = ((EARLY, EARLY + 4), (EARLY + 4, EARLY + 8), (EARLY + 8, len(late)))

        def prep_bank(u):
            return bank[u % 8] if u < U1 else bank[5 + (u - U1) % 3]

        def emptied(eng, u):
            eng.wait_ge(prep_out, u + 1)

        def empty_prep(act, lo, hi):
            for u in range(lo, hi):
                b = prep_bank(u)
                act.wait_ge(prep_filled, u + 1)
                if u < U1:
                    c = nc.scalar.copy(cw[:, u, :], b[:, 0:PAIRS])
                else:
                    src, dst, rows = late[u - U1]
                    n = len(src)
                    if n > 1:
                        c = nc.scalar.copy(dst, b[0:rows, 0:n * P].rearrange("r (n h) -> r n h", n=n))
                    else:
                        c = nc.scalar.copy(dst, b[0:rows, 0:P])
                c.then_inc(prep_out, 1)


        block = ctx.enter_context(nc.Block())

        @block.sync
        def _(sp):
            sp.dma_start(ids_sb[:, :, :], ids.rearrange("(t p) f -> p t f", p=P)).then_inc(ids_loaded, 16)
            sp.dma_start(w1raw[:, :, :], W1).then_inc(w1_loaded, 16)
            sp.dma_start(w1s[:, ONE:ONE + 1], b1.rearrange("(p o) -> p o", o=1)).then_inc(w1_loaded, 16)
            for n, c in enumerate((slice(0, NA), slice(NA, F))):
                sp.dma_start(w2t[:, c, :], W2[:, c, :]).then_inc(w2_loaded[n], 16)
            sp.dma_start(dense_t[:, :, :], dense).then_inc(dense_loaded, 16)
            sp.dma_start(wt1[:, :, :], W_top1[0:2 * H, :].rearrange("(c p) n -> p c n", p=P)).then_inc(tower_loaded, 16)
            sp.dma_start(wt1d[:, :], W_top1[2 * H:2 * H + ND, :]).then_inc(tower_loaded, 16)
            sp.dma_start(wt2[:, :, :], W_top2.rearrange("(p m) n -> p m n", m=M1)).then_inc(tower_loaded, 16)
            sp.dma_start(wt3[:, :], W_top3.rearrange("(p m) o -> p (m o)", m=M2)).then_inc(tower_loaded, 16)
            sp.dma_start(bt1[:, :], b_top1.rearrange("(p m) -> p m", m=M1)).then_inc(tower_loaded, 16)
            sp.dma_start(bt2[:, :], b_top2.rearrange("(p m) -> p m", m=M2)).then_inc(tower_loaded, 16)
            sp.dma_start(b2s[:, 0:1], b2.rearrange("(p o) -> p o", o=1)).then_inc(tower_loaded, 16)
            sp.wait_ge(tile_out, TILES)
            sp.dma_start(out.rearrange("(a n) o -> a (n o)", a=1),
                         ys[:, :, :, :].rearrange("a t g s -> a (t g s)")).then_inc(stored, 16)
            sp.wait_ge(stored, 16)

        @block.gpsimd
        def _(pool):
            nc.gpsimd.memset(ident[:, :], 0.0).then_inc(ident_zero, 1)
            pool.wait_ge(ident_zero, 1)
            nc.gpsimd.affine_select(out=ident[:, :], in_=ident[:, :], compare_op=ALU.not_equal, fill=1.0,
                                    base=0, pattern=[[-1, P]], channel_multiplier=1).then_inc(ident_ready, 1)
            pool.wait_ge(ids_loaded, 16)
            for t in range(TILES):
                for n, (f0, fields, _, _) in enumerate(PARTS):
                    if t >= 2:
                        pool.wait_ge(x_transposed, NP * (t - 2) + n + 1)
                        pool.wait_ge(pair_summed, STEPS * (t - 1))
                    for f in range(f0, f0 + fields):
                        pool.indirect_dma_start(gathered[:, t % 2, f, :], None, tables[f],
                                                bass.IndirectOffsetOnAxis(ids_sb[:, t, f:f + 1], axis=0)
                                                ).then_inc(gathered_in[n][t % 2], 16)

        @block.tensor
        def _(pe):
            def weight_transposes(lo, hi):
                for v in range(lo, hi):
                    srcs, _, rows = late[v]
                    u = U1 + v
                    if v >= 3:
                        emptied(pe, u - 3)
                    for n, src in enumerate(srcs):
                        last = nc.tensor.transpose(prep_bank(u)[0:rows, n * P:(n + 1) * P], src, ident[:, :])
                    last.then_inc(prep_filled, 1)

            def warm_up(n, b=0):
                for _ in range(n):
                    nc.tensor.matmul(bank[b][:, 0:P], ident[:, :], ident[:, :], start=True, stop=True)

            pe.wait_ge(ident_ready, 1)
            warm_up(WARM)
            pe.wait_ge(w1_ready, 1)
            for c in range(F):
                if c in (0, NA):
                    pe.wait_ge(w2_loaded[c // NA], 16)
                if c >= 8:
                    emptied(pe, c - 8)
                if c == NA:
                    pe.wait_ge(w1_ready, 2)
                nc.tensor.matmul(prep_bank(c)[:, 0:PAIRS], w2t[:, c, :], (w1sb if NA <= c < NAB else w1s)[:, :],
                                 start=True, stop=True).then_inc(prep_filled, 1)
            pe.wait_ge(tower_loaded, 16 * 7)
            pe.wait_ge(dense_loaded, 16)
            for m in range(M1):
                emptied(pe, U1 - 8 + m)
                nc.tensor.matmul(bank[(U1 + m) % 8][:, 0:BATCH], at(wt1d, m, (M1, P), rows=ND),
                                 at(dense_t, 0, (1, BATCH), rows=ND), start=True, stop=True).then_inc(hd_done, 1)
            emptied(pe, U1 - 1)
            warm_up(WARM_HD)
            pe.wait_ge(hd_out, M1)
            weight_transposes(0, EARLY)
            warm_up(WARM_TILE)

            def moments(t, lo, hi):
                d, px, py = xdiag[t % 2], prodx[t % 2], prody[t % 2]
                pe.wait_ge(diag_ready, NP * (t + 1))
                pe.wait_ge(prod_ready, NP * (t + 1))
                for u in range(lo, hi):
                    n = XU * t + u
                    if n >= 3:
                        pe.wait_ge(x_out, n - 2)
                    for i in range(XG):
                        mx = nc.tensor.matmul(bank[n % 3][0:XR, i * NX:(i + 1) * NX],
                                              at(px, u * XG + i, (Q, XR)),
                                              at(d, u * XG + i, (J * Q, G), (Q, JXS)), start=True, stop=True)
                    mx.then_inc(x_filled, 1)
                    if n >= 2:
                        pe.wait_ge(y_out, n - 1)
                    for i in range(YG):
                        my = nc.tensor.matmul(bank[3 + n % 2][0:AB, i * NY:(i + 1) * NY],
                                              at(py, u * YG + i, (Q, AB)),
                                              at(d, (J - JYS) * Q + u * YG + i, (J * Q, G), (Q, JYS)),
                                              start=True, stop=True)
                    my.then_inc(y_filled, 1)

            def cin(t):
                pe.wait_ge(x_out, XU * (t + 1))
                pe.wait_ge(y_out, YU * (t + 1))
                z1, z2 = bank[Z1][:, 0:P], bank[Z2][:, 0:P]
                nc.tensor.matmul(z1, zwx[0:XR, :], tx[0:XR, F, :], start=True, stop=False)
                nc.tensor.matmul(z1, zwab[0:AB, :], ty[0:AB, NC, :], start=False, stop=False)
                if t:
                    tower3(t - 1)
                else:
                    emptied(pe, U - 1)
                terms = [(cx[0:XR, j, :], tx[0:XR, j, :]) for j in range(F)]
                terms += [(cy[0:AB, c, :], ty[0:AB, c, :]) for c in range(NC)]
                for n, (w, m) in enumerate(terms):
                    if n == PAIRS_AT:
                        pe.wait_ge(pair_summed, STEPS * (t + 1))
                        for i in range(2):
                            last = nc.tensor.transpose(bank[ZP][0:AC, i * P:(i + 1) * P],
                                                       pair_sum[:, i * AC:(i + 1) * AC], ident[:, :])
                        last.then_inc(pair_filled, 1)
                    if n == PAIRS_AT + 8:
                        pe.wait_ge(pair_out, t + 1)
                        for i in range(2):
                            last = nc.tensor.matmul(z1, zwc[0:AC, i, :], pair_rows[0:AC, i, :],
                                                    start=False, stop=(i == 1))
                        last.then_inc(z_done, 1)
                    last = nc.tensor.matmul(z2, w, m, start=(n == 0), stop=(n == len(terms) - 1))
                last.then_inc(z_done, 1)
                pe.wait_ge(z_out, 2 * t + 1)

            def hidden_block(m, c):
                h = bank[(H1A, H1B)[2 * m // M1]][:, (m % 2) * P:(m % 2 + 1) * P]
                return nc.tensor.matmul(h, at(wt1, c * N1 + m, (M1, P)), zs[:, c, :], start=(c == 0), stop=(c == 1))

            def tower1_start(t):
                if t:
                    pe.wait_ge(tile_out, t)
                    pe.wait_ge(h2_act, t)
                for m in range(0, M1, 2):
                    hidden_block(m, 0)

            def tower1(t):
                pe.wait_ge(z_out, 2 * (t + 1))
                for m in range(0, M1, 2):
                    hidden_block(m, 1)
                    hidden_block(m + 1, 0)
                    hidden_block(m + 1, 1).then_inc(h1_done, 1)

            def tower2(t, m):
                pe.wait_ge(h1_dve, t + 1)
                h = bank[(H1A, H1B)[m]][:, 2 * P:3 * P]
                for c in range(M1):
                    last = nc.tensor.matmul(h, at(wt2, c * N2 + m, (M2, P)), h1s[:, c, :],
                                            start=(c == 0), stop=(c == M1 - 1))
                last.then_inc(h2_done, 1)

            def tower3(t):
                pe.wait_ge(h2_act, t + 1)
                pe.wait_ge(h2_dve, t + 1)
                for c in range(M2):
                    last = nc.tensor.matmul(bank[H1A][0:1, 3 * P:4 * P], wt3[:, c:c + 1], h2s[:, c, :],
                                            start=(c == 0), stop=(c == M2 - 1))
                last.then_inc(y_done, 1)

            for n in range(4):
                moments(0, n * XU // 4, (n + 1) * XU // 4)
                if n == 1:
                    pe.wait_ge(orders_added, 4)
                if n:
                    weight_transposes(*LATE_PARTS[n - 1])
            cin(0)
            for t in range(1, TILES):
                tower1_start(t - 1)
                if t < TILES - 1:
                    warm_up(WARM_T[t], 2)
                    moments(t, 0, XU // 4)
                    tower1(t - 1)
                    moments(t, XU // 4, XU // 2)
                    tower2(t - 1, 0)
                    moments(t, XU // 2, XU)
                else:
                    tower1(t - 1)
                    moments(t, 0, XU // 4)
                    tower2(t - 1, 0)
                    moments(t, XU // 4, XU)
                tower2(t - 1, 1)
                cin(t)
            t = TILES - 1
            pe.wait_ge(tile_out, t)
            for m in range(M1):
                h = bank[LAST1[m]][:, 0:P]
                nc.tensor.matmul(h, at(wt1, m, (M1, P)), zs[:, 0, :], start=True, stop=False)
            pe.wait_ge(z_out, 2 * t + 2)
            for m in range(M1):
                nc.tensor.matmul(bank[LAST1[m]][:, 0:P], at(wt1, N1 + m, (M1, P)), zs[:, 1, :],
                                 start=False, stop=True).then_inc(h1_done, 1)
            for c in range(M1):
                if c % 2:
                    pe.wait_ge(h1_dve, t + c // 2 + 1)
                else:
                    pe.wait_ge(h1_act, c // 2 + 1)
                for m in range(M2):
                    last = nc.tensor.matmul(bank[LAST2[m]][:, 0:P], at(wt2, c * N2 + m, (M2, P)), h1s[:, c, :],
                                            start=(c == 0), stop=(c == M1 - 1))
                    if c == M1 - 1:
                        last.then_inc(h2_done, 1)
            for c in range(M2):
                pe.wait_ge((h2_act, h2_dve)[c], t + 1)
                last = nc.tensor.matmul(bank[LAST3][0:1, 0:P], wt3[:, c:c + 1], h2s[:, c, :],
                                        start=(c == 0), stop=(c == M2 - 1))
            last.then_inc(y_done, 1)

        @block.scalar
        def _(act):
            def diagonal(t, n):
                d, x = xdiag[t % 2], xk[:, t % 2, :, :]
                f0, fields, _, _ = PARTS[n]
                if t < 2 and n == 0:
                    act.wait_ge(consts_ready, t + 1)
                if t >= 2 and n == 0:
                    act.wait_ge(y_filled, YU * (t - 1))
                act.wait_ge(x_transposed, NP * t + n + 1)
                for g in range(G):
                    last = nc.scalar.copy(d[g * Q:(g + 1) * Q, g * J + f0:g * J + f0 + fields, :],
                                          x[g * Q:(g + 1) * Q, f0:f0 + fields, :])
                last.then_inc(diag_ready, 1)

            def sums(t, lo, hi):
                for u in range(lo, hi):
                    n = XU * t + u
                    act.wait_ge(x_filled, n + 1)
                    if t and u == 0:
                        act.wait_ge(z_done, 2 * t)
                    nc.scalar.copy(
                        tx[0:XR, :, u * XG * G:(u + 1) * XG * G].rearrange("r j (s g) -> r s g j", s=XG),
                        bank[n % 3][0:XR, :].rearrange("r (s g j) -> r s g j", s=XG, g=G)[:, :, :, 0:J]
                    ).then_inc(x_out, 1)
                    act.wait_ge(y_filled, n + 1)
                    nc.scalar.copy(
                        ty[0:AB, :, u * YG * G:(u + 1) * YG * G].rearrange("r j (s g) -> r s g j", s=YG),
                        bank[3 + n % 2][0:AB, 0:YG * NY].rearrange("r (s g j) -> r s g j", s=YG, g=G)
                        [:, :, :, JYS - JY:JYS]
                    ).then_inc(y_out, 1)

            def z_rows(t, i):
                if i == 0:
                    act.wait_ge(pair_filled, t + 1)
                    nc.scalar.copy(pair_rows[0:AC, :, :].rearrange("r i (s g) -> r i g s", g=G),
                                   bank[ZP][0:AC, 0:2 * P].rearrange("r (i g s) -> r i g s", i=2, g=G)
                                   ).then_inc(pair_out, 1)
                    act.wait_ge(z_done, 2 * t + 1)
                    nc.scalar.copy(zs[:, 0, :], bank[Z1][:, 0:P]).then_inc(z_out, 1)
                else:
                    if t == 0:
                        act.wait_ge(b2_scaled, 1)
                    act.wait_ge(z_done, 2 * t + 2)
                    nc.scalar.activation(zs[:, 1, :], bank[Z2][:, 0:P], ACT.Identity,
                                         bias=b2s[:, 1:2]).then_inc(z_out, 1)

            def hidden2(t):
                act.wait_ge(h2_done, 2 * t + 2)
                nc.scalar.activation(h2s[:, 1, :], bank[H1B][:, 2 * P:3 * P], ACT.Relu,
                                     bias=bt2[:, 1:2]).then_inc(h2_act, 1)

            def result(t, src):
                act.wait_ge(y_done, t + 1)
                nc.scalar.copy(ys[:, t, :, :], src.rearrange("a (s g) -> a g s", g=G)
                               ).then_inc(tile_out, 1)

            empty_prep(act, 0, NAB)
            diagonal(0, 0)
            empty_prep(act, NAB, U1)
            diagonal(0, 1)
            act.wait_ge(tower_loaded, 16 * 7)
            for m in range(M1):
                act.wait_ge(hd_done, m + 1)
                nc.scalar.activation(hd[:, m, :], bank[(U1 + m) % 8][:, 0:BATCH], ACT.Identity,
                                     bias=bt1[:, m:m + 1]).then_inc(hd_out, 1)
            empty_prep(act, U1, U1 + EARLY)
            for n in range(2, NP):
                diagonal(0, n)
            for n in range(4):
                sums(0, n * XU // 4, (n + 1) * XU // 4)
                if n:
                    empty_prep(act, U1 + LATE_PARTS[n - 1][0], U1 + LATE_PARTS[n - 1][1])
            for t in range(1, TILES):
                if t >= 2:
                    result(t - 2, bank[H1A][0:1, 3 * P:4 * P])
                diagonal(t, 0)
                diagonal(t, 1)
                z_rows(t - 1, 0)
                diagonal(t, 2)
                z_rows(t - 1, 1)
                diagonal(t, 3)
                sums(t, 0, XU)
                hidden2(t - 1)
            t = TILES - 1
            result(t - 1, bank[H1A][0:1, 3 * P:4 * P])
            z_rows(t, 0)
            z_rows(t, 1)
            for m in range(0, M1, 2):
                act.wait_ge(h1_added, 2 * t + m + 1)
                nc.scalar.activation(h1s[:, m, :], at(h1sum, m * P, (1, P)), ACT.Relu).then_inc(h1_act, 1)
            act.wait_ge(h2_done, 2 * t + 1)
            nc.scalar.activation(h2s[:, 0, :], bank[LAST2[0]][:, 0:P], ACT.Relu,
                                 bias=bt2[:, 0:1]).then_inc(h2_act, 1)
            result(t, bank[LAST3][0:1, 0:P])

        @block.vector
        def _(dve):
            def constants(i):
                nc.vector.memset(xdiag[i][:, :, :], 0.0).then_inc(zeroed, 1)
                nc.vector.memset(prodx[i][:, ONE, :], 1.0)
                dve.wait_ge(zeroed, i + 1)
                for g in range(G):
                    last = nc.vector.memset(xdiag[i][g * Q:(g + 1) * Q, g * J + F, :], 1.0)
                last.then_inc(consts_ready, 1)

            constants(0)
            dve.wait_ge(w1_loaded, 32)
            nc.vector.tensor_tensor(w1both[:, :, :], w1raw[:, :, :], w1raw[:, :, :].rearrange("h p q -> h q p"),
                                    ALU.add).then_inc(w1_step, 1)
            dve.wait_ge(w1_step, 1)
            nc.vector.tensor_copy(at(w1both, 0, (F + 1, F)), at(w1raw, 0, (F + 1, F))).then_inc(w1_step, 1)
            dve.wait_ge(w1_step, 2)
            for q in range(NA):
                nc.vector.tensor_copy(at(w1s, tri(q), (TA, 2), (1, q + 1)),
                                      at(w1both, q * F, (NA * (F + 1), 2), (1, q + 1)))
            for q in range(NC):
                nc.vector.tensor_copy(at(w1s, 2 * TA + tri(q), (1, q + 1)),
                                      at(w1both, (NAB + q) * F + NAB, (1, q + 1)))
            nc.vector.tensor_copy(at(w1s, CAB, (NA, NA), (1, NA)), at(w1both, NA, (F, NA), (1, NA)))
            nc.vector.tensor_copy(at(w1s, CPC, (NC, NAB), (1, NC)),
                                  at(w1both, NAB, (F, NAB), (1, NC))).then_inc(w1_ready, 1)
            dve.wait_ge(w1_ready, 1)
            nc.vector.tensor_copy(w1sb[:, :], w1s[:, :]).then_inc(w1_step, 1)
            dve.wait_ge(w1_step, 3)
            nc.vector.tensor_copy(at(w1sb, CAB, (NA, NA), (1, NA)),
                                  at(w1both, NA * F, (F, NA), (1, NA))).then_inc(w1_ready, 1)
            constants(1)
            dve.wait_ge(tower_loaded, 16 * 7)
            nc.vector.tensor_scalar(b2s[:, 1:2], b2s[:, 0:1], float(E), None, ALU.mult).then_inc(b2_scaled, 1)

            def add_orders(step):
                second = step >= 2
                other_q = step % 2 == 0
                if other_q:
                    emptied(dve, F - 1 if second else NAB - 1)
                else:
                    dve.wait_ge(orders_added, step)

                def add(dst, src, dims_dst, dims_src):
                    d = at(cw, dst, *dims_dst)
                    return nc.vector.tensor_tensor(d, d, at(cw, src, *dims_src), ALU.add)

                for q in range(NA):
                    n = q + 1 if other_q else q
                    if not n:
                        continue
                    if not second:
                        off, st = (q * PAIRS + CAB, NA) if other_q else (CAB + NA * q, PAIRS)
                        last = add(NA * PAIRS + tri(q), off, ((TA - NA * PAIRS, 2), (PAIRS, NA), (1, n)),
                                   ((NA * PAIRS, 2), (1, NA), (st, n)))
                    else:
                        off, st = (q * PAIRS + CPC, NC) if other_q else (CPC + NC * q, PAIRS)
                        last = add(NAB * PAIRS + tri(q), off, ((TA, 2), (PAIRS, NC), (1, n)),
                                   ((NA * PAIRS + NA * NC, 2), (1, NC), (st, n)))
                if second:
                    for q in range(NC):
                        n = q + 1 if other_q else q
                        if n:
                            off, st = (((NAB + q) * PAIRS + CPC, 1) if other_q else (NAB * PAIRS + CPC + q, PAIRS))
                            last = add(2 * TA + tri(q), off, ((PAIRS, NAB), (1, n)), ((NC, NAB), (st, n)))
                    if other_q:
                        last = add(NAB * PAIRS + CAB, NA * PAIRS + CPC, ((NA, NA), (1, NA), (PAIRS, NC)),
                                   ((NC, NA), (PAIRS, NA), (1, NC)))
                    else:
                        last = add(NAB * PAIRS + CAB, CPC + NA * NC, ((NA, NA), (1, NA), (PAIRS, NC)),
                                   ((PAIRS, NA), (NC, NA), (1, NC)))
                last.then_inc(orders_added, 1)

            def transposed(t, n):
                b = t % 2
                f0, fields, _, _ = PARTS[n]
                dve.wait_ge(gathered_in[n][b], 16 * fields * (t // 2 + 1))
                if t >= 2:
                    dve.wait_ge(diag_ready, NP * (t - 2) + n + 1)
                x0 = (b * F + f0) * Q
                nc.vector.transpose(at(xk, x0, (1, fields * Q)), at(gathered, x0, (1, fields * Q))
                                    ).then_inc(x_transposed, 1)

            def products(t, n):
                b = t % 2
                f0, fields, block0, row0 = PARTS[n]
                x0 = (b * F + block0) * Q
                dve.wait_ge(x_transposed, NP * t + n + 1)
                if t >= 2:
                    dve.wait_ge(y_filled, YU * (t - 1))
                for q in range(f0 - block0, f0 - block0 + fields):
                    last = nc.vector.tensor_tensor(at(prodx[b], (row0 + tri(q)) * Q, (Q, q + 1), (1, Q)),
                                                   at(xk, x0, (Q, q + 1), (1, Q)),
                                                   at(xk, x0 + q * Q, (0, q + 1), (1, Q)), ALU.mult)
                if n == 1:
                    last = nc.vector.tensor_tensor(at(prody[b], 0, (NA * Q, NA), (Q, NA), (1, Q)),
                                                   at(xk, x0 - NA * Q, (Q, NA), (0, NA), (1, Q)),
                                                   at(xk, x0, (0, NA), (Q, NA), (1, Q)), ALU.mult)
                last.then_inc(prod_ready, 1)

            def pair_sums(t, step1=None, step2=None):
                if t:
                    dve.wait_ge(pair_filled, t)
                b0 = t % 2 * F

                def multiply(i):
                    n = STEPS * t + i
                    if n >= 2:
                        dve.wait_ge(pair_summed, n - 1)
                    nc.vector.tensor_tensor(at(pair_prod[n % 2], 0, (NC * E, PC), (E, NC), (1, E)),
                                            at(gathered, (b0 + i * PC) * E, (E, PC), (0, NC), (1, E)),
                                            at(gathered, (b0 + NAB) * E, (0, PC), (E, NC), (1, E)), ALU.mult
                                            ).then_inc(pair_multiplied, 1)

                multiply(0)
                for i in range(STEPS):
                    if i == step1:
                        hidden1(t - 1)
                    if i == step2:
                        hidden2(t - 1)
                    if i + 1 < STEPS:
                        multiply(i + 1)
                    n = STEPS * t + i
                    dve.wait_ge(pair_multiplied, n + 1)
                    nc.vector.tensor_reduce(pair_sum[:, i * PC * NC:(i + 1) * PC * NC], pair_prod[n % 2][:, :, :],
                                            mybir.AxisListType.X, ALU.add).then_inc(pair_summed, 1)

            def hidden1(t):
                half = M1 // 2
                for i, b in enumerate((H1A, H1B)):
                    dve.wait_ge(h1_done, 2 * t + i + 1)
                    nc.vector.tensor_tensor(at(h1sum, i * half * P, (P, half), (1, P)),
                                            bank[b][:, 0:half * P].rearrange("p (m s) -> p m s", m=half),
                                            hd[:, i * half:(i + 1) * half, t * P:(t + 1) * P], ALU.add
                                            ).then_inc(h1_added, 1)
                dve.wait_ge(h1_added, 2 * t + 2)
                nc.vector.tensor_scalar(at(w1both, 0, (1, M1 * P)), at(h1sum, 0, (1, M1 * P)), 0.0, None, ALU.max
                                        ).then_inc(h1_dve, 1)

            def hidden2(t):
                dve.wait_ge(h2_done, 2 * t + 1)
                nc.vector.tensor_scalar(h2s[:, 0, :], bank[H1A][:, 2 * P:3 * P], bt2[:, 0:1], 0.0,
                                        ALU.add, ALU.max).then_inc(h2_dve, 1)

            transposed(0, 0)
            products(0, 0)
            add_orders(0)
            add_orders(1)
            for n in range(1, NP):
                transposed(0, n)
                products(0, n)
            add_orders(2)
            add_orders(3)
            pair_sums(0)
            for t in range(1, TILES):
                for n in range(NP):
                    transposed(t, n)
                    products(t, n)
                if t < TILES - 1:
                    pair_sums(t, 3, 5)
                else:
                    pair_sums(t, 0, 3)
            t = TILES - 1
            for m in range(M1):
                dve.wait_ge(h1_done, 2 * t + m + 1)
                nc.vector.tensor_tensor(at(h1sum, m * P, (1, P)), bank[LAST1[m]][:, 0:P],
                                        hd[:, m, t * P:(t + 1) * P], ALU.add).then_inc(h1_added, 1)
                if m % 2:
                    dve.wait_ge(h1_added, 2 * t + m + 1)
                    nc.vector.tensor_scalar(h1s[:, m, :], at(h1sum, m * P, (1, P)), 0.0, None, ALU.max
                                            ).then_inc(h1_dve, 1)
            dve.wait_ge(h2_done, 2 * t + 2)
            nc.vector.tensor_scalar(h2s[:, 1, :], bank[LAST2[1]][:, 0:P], bt2[:, 1:2], 0.0,
                                    ALU.add, ALU.max).then_inc(h2_dve, 1)


_INS = (["dense_ctx", "ids"] + [f"tbl_{f}" for f in range(26)] +
        ["W_top1", "b_top1", "W_top2", "b_top2", "W_top3", "L0_rec_W1", "L0_rec_b1", "L0_rec_W2", "L0_rec_b2"])


def kernel(**inputs):
    import numpy as _np
    import concourse.bacc as _bacc
    from concourse import mybir as _mybir
    from concourse.bass_utils import run_bass_kernel_spmd as _run

    nc = _bacc.Bacc("TRN2", target_bir_lowering=False, num_devices=1)
    arrays, aps = {}, {}
    for name in _INS:
        a = _np.asarray(inputs[name])
        if name == "L0_rec_W2":
            a = a.transpose(1, 2, 0)
        if name == "dense_ctx":
            a = a.reshape(-1, 4, 32, a.shape[1]).transpose(3, 0, 2, 1).reshape(a.shape[1], -1, 128)
        a = _np.ascontiguousarray(a)
        arrays[f"in_{name}"] = a
        aps[name] = nc.dram_tensor(f"in_{name}", a.shape, _mybir.dt.from_np(a.dtype), kind="ExternalInput").ap()
    out = nc.dram_tensor("out_y", (inputs["ids"].shape[0], 1), _mybir.dt.float32, kind="ExternalOutput").ap()
    build(nc, aps["dense_ctx"], aps["ids"], [aps[f"tbl_{f}"] for f in range(26)], aps["W_top1"], aps["b_top1"],
          aps["W_top2"], aps["b_top2"], aps["W_top3"], aps["L0_rec_W1"], aps["L0_rec_b1"], aps["L0_rec_W2"],
          aps["L0_rec_b2"], out)
    r = _run(nc, [arrays], core_ids=[0])
    return r.results[0]["out_y"]
```
